# Optimizing a Trainium2 kernel written in Bass

```python
import numpy as np
import jax
import jax.numpy as jnp

def _softmax(x, axis=-1):
    return jax.nn.softmax(x, axis=axis)

def _gelu(x):
    return jax.nn.gelu(x, approximate=True)

def _silu(x):
    return jax.nn.silu(x)

def _sigmoid(x):
    return jax.nn.sigmoid(x)

def _layernorm(x, axis=-1, eps=1e-05):
    m = jnp.mean(x, axis=axis, keepdims=True)
    v = jnp.var(x, axis=axis, keepdims=True)
    return (x - m) / jnp.sqrt(v + eps)

def _scatter_add(tgt, idx, src, axis=0):
    return tgt.at[idx].add(src)

def _segment_sum(src, seg, n):
    return jax.ops.segment_sum(src, seg, n)
kernel_name = 'mk_metaformer_d1_conv_nchw1024_r2_adc235'

def setup_inputs(seed: int=0):
    np.random.seed(seed)
    _w = jnp.asarray

    def _rec_inputs():
        import jax
        import jax.numpy as jnp
        _gk = jax.random.key(seed)
        x = -0.0006537 + 1.001 * jax.random.normal(jax.random.fold_in(_gk, 1), (4, 512, 24, 24), jnp.float32)
        return x
    x = _rec_inputs()

    def _L0_conv_setup():
        import jax, jax.numpy as jnp
        import numpy as np
        DIM = 512
        R = 2
        D_MODEL = DIM // (R * R)
        D_INNER = 2 * D_MODEL
        D_STATE = 16
        D_CONV = 4
        DT_RANK = (D_MODEL + 15) // 16
        NUM_TOKENS = 1

        def pixel_shuffle(x, r):
            B, C, H, W = x.shape
            c = C // (r * r)
            x = x.reshape(B, c, r, r, H, W)
            x = x.transpose(0, 1, 4, 2, 5, 3)
            return x.reshape(B, c, H * r, W * r)

        def pixel_unshuffle(x, r):
            B, C, Hr, Wr = x.shape
            H, W = (Hr // r, Wr // r)
            x = x.reshape(B, C, H, r, W, r)
            x = x.transpose(0, 1, 3, 5, 2, 4)
            return x.reshape(B, C * r * r, H, W)

        def mamba_block(seq, in_proj_w, conv_w, conv_b, x_proj_w, dt_proj_w, dt_proj_b, A_log, D, out_proj_w):
            B, L, _ = seq.shape
            xz = jnp.einsum('bld,ed->ble', seq, in_proj_w)
            u, z = jnp.split(xz, 2, axis=-1)
            up = jnp.pad(u, ((0, 0), (D_CONV - 1, 0), (0, 0)))
            u = sum((up[:, k:k + L, :] * conv_w[:, k] for k in range(D_CONV))) + conv_b
            u = jax.nn.silu(u)
            x_dbl = jnp.einsum('bld,ed->ble', u, x_proj_w)
            dt, Bm, Cm = jnp.split(x_dbl, [DT_RANK, DT_RANK + D_STATE], axis=-1)
            dt = jax.nn.softplus(jnp.einsum('blr,dr->bld', dt, dt_proj_w) + dt_proj_b)
            A = -jnp.exp(A_log)

            def step(h, inputs):
                dt_t, B_t, C_t, u_t = inputs
                dA = jnp.exp(dt_t[:, :, None] * A)
                h = dA * h + (dt_t * u_t)[:, :, None] * B_t[:, None, :]
                y = jnp.einsum('bdn,bn->bd', h, C_t)
                return (h, y)
            h0 = jnp.zeros((B, D_INNER, D_STATE), dtype=seq.dtype)
            xs = (dt.transpose(1, 0, 2), Bm.transpose(1, 0, 2), Cm.transpose(1, 0, 2), u.transpose(1, 0, 2))
            _, ys = jax.lax.scan(step, h0, xs)
            y = ys.transpose(1, 0, 2) + u * D
            y = y * jax.nn.silu(z)
            return jnp.einsum('bld,ed->ble', y, out_proj_w)
        key = jax.random.key(seed)
        ks = jax.random.split(key, 12)
        s = lambda k, shape, scale=0.02: jax.random.normal(k, shape, dtype=jnp.float32) * scale
        inp = {'x': jax.random.normal(ks[0], (4, DIM, 24, 24), dtype=jnp.float32), 'global_token': jnp.zeros((1, NUM_TOKENS, D_MODEL), dtype=jnp.float32), 'in_proj_w': s(ks[1], (2 * D_INNER, D_MODEL)), 'conv_w': s(ks[2], (D_INNER, D_CONV), 0.1), 'conv_b': jnp.zeros((D_INNER,), dtype=jnp.float32), 'x_proj_w': s(ks[3], (DT_RANK + 2 * D_STATE, D_INNER)), 'dt_proj_w': s(ks[4], (D_INNER, DT_RANK), 0.1), 'dt_proj_b': jax.random.uniform(ks[5], (D_INNER,), dtype=jnp.float32, minval=-4.0, maxval=-2.0), 'A_log': jnp.log(jnp.broadcast_to(jnp.arange(1, D_STATE + 1, dtype=jnp.float32), (D_INNER, D_STATE))), 'D': jnp.ones((D_INNER,), dtype=jnp.float32), 'out_proj_w': s(ks[6], (D_MODEL, D_INNER))}
        return inp
    _L0_conv_all = _L0_conv_setup()
    _L0_conv_in = {k: v for k, v in _L0_conv_all.items() if k in ('global_token', 'in_proj_w', 'conv_w', 'conv_b', 'x_proj_w', 'dt_proj_w', 'dt_proj_b', 'A_log', 'D', 'out_proj_w')}
    del _L0_conv_all

    def _L0_ffn_setup():
        import jax, jax.numpy as jnp
        import numpy as np
        TOP_K = 8
        key = jax.random.key(seed)
        k1, k2, k3 = jax.random.split(key, 3)
        B, S, D = (16, 1024, 512)
        M, T = (256, 128)
        x = jax.random.normal(k1, (B, S, D), dtype=jnp.float32)
        memory_tokens = jax.random.normal(k2, (M, T, D), dtype=jnp.float32) * 0.02
        memory_router = jax.random.normal(k3, (D, M), dtype=jnp.float32) * 0.02
        return {'x': x, 'memory_tokens': memory_tokens, 'memory_router': memory_router}
    _L0_ffn_all = _L0_ffn_setup()
    _L0_ffn_in = {k: v for k, v in _L0_ffn_all.items() if k in ('memory_tokens', 'memory_router')}
    del _L0_ffn_all
    return {'x': x, 'L0_conv_global_token': _L0_conv_in['global_token'], 'L0_conv_in_proj_w': _L0_conv_in['in_proj_w'], 'L0_conv_conv_w': _L0_conv_in['conv_w'], 'L0_conv_conv_b': _L0_conv_in['conv_b'], 'L0_conv_x_proj_w': _L0_conv_in['x_proj_w'], 'L0_conv_dt_proj_w': _L0_conv_in['dt_proj_w'], 'L0_conv_dt_proj_b': _L0_conv_in['dt_proj_b'], 'L0_conv_A_log': _L0_conv_in['A_log'], 'L0_conv_D': _L0_conv_in['D'], 'L0_conv_out_proj_w': _L0_conv_in['out_proj_w'], 'L0_ffn_memory_tokens': _L0_ffn_in['memory_tokens'], 'L0_ffn_memory_router': _L0_ffn_in['memory_router']}

def reference(x, L0_conv_global_token, L0_conv_in_proj_w, L0_conv_conv_w, L0_conv_conv_b, L0_conv_x_proj_w, L0_conv_dt_proj_w, L0_conv_dt_proj_b, L0_conv_A_log, L0_conv_D, L0_conv_out_proj_w, L0_ffn_memory_tokens, L0_ffn_memory_router):
    import jax
    import jax.numpy as jnp

    def _L0_conv_ref(x, global_token, in_proj_w, conv_w, conv_b, x_proj_w, dt_proj_w, dt_proj_b, A_log, D, out_proj_w):
        import jax, jax.numpy as jnp
        import numpy as np
        DIM = 512
        R = 2
        D_MODEL = DIM // (R * R)
        D_INNER = 2 * D_MODEL
        D_STATE = 16
        D_CONV = 4
        DT_RANK = (D_MODEL + 15) // 16
        NUM_TOKENS = 1

        def pixel_shuffle(x, r):
            B, C, H, W = x.shape
            c = C // (r * r)
            x = x.reshape(B, c, r, r, H, W)
            x = x.transpose(0, 1, 4, 2, 5, 3)
            return x.reshape(B, c, H * r, W * r)

        def pixel_unshuffle(x, r):
            B, C, Hr, Wr = x.shape
            H, W = (Hr // r, Wr // r)
            x = x.reshape(B, C, H, r, W, r)
            x = x.transpose(0, 1, 3, 5, 2, 4)
            return x.reshape(B, C * r * r, H, W)

        def mamba_block(seq, in_proj_w, conv_w, conv_b, x_proj_w, dt_proj_w, dt_proj_b, A_log, D, out_proj_w):
            B, L, _ = seq.shape
            xz = jnp.einsum('bld,ed->ble', seq, in_proj_w)
            u, z = jnp.split(xz, 2, axis=-1)
            up = jnp.pad(u, ((0, 0), (D_CONV - 1, 0), (0, 0)))
            u = sum((up[:, k:k + L, :] * conv_w[:, k] for k in range(D_CONV))) + conv_b
            u = jax.nn.silu(u)
            x_dbl = jnp.einsum('bld,ed->ble', u, x_proj_w)
            dt, Bm, Cm = jnp.split(x_dbl, [DT_RANK, DT_RANK + D_STATE], axis=-1)
            dt = jax.nn.softplus(jnp.einsum('blr,dr->bld', dt, dt_proj_w) + dt_proj_b)
            A = -jnp.exp(A_log)

            def step(h, inputs):
                dt_t, B_t, C_t, u_t = inputs
                dA = jnp.exp(dt_t[:, :, None] * A)
                h = dA * h + (dt_t * u_t)[:, :, None] * B_t[:, None, :]
                y = jnp.einsum('bdn,bn->bd', h, C_t)
                return (h, y)
            h0 = jnp.zeros((B, D_INNER, D_STATE), dtype=seq.dtype)
            xs = (dt.transpose(1, 0, 2), Bm.transpose(1, 0, 2), Cm.transpose(1, 0, 2), u.transpose(1, 0, 2))
            _, ys = jax.lax.scan(step, h0, xs)
            y = ys.transpose(1, 0, 2) + u * D
            y = y * jax.nn.silu(z)
            return jnp.einsum('bld,ed->ble', y, out_proj_w)
        B, C, H, W = x.shape
        xs = pixel_shuffle(x, R)
        seq = xs.reshape(B, D_MODEL, -1).transpose(0, 2, 1)
        tok = jnp.broadcast_to(global_token, (B, NUM_TOKENS, D_MODEL))
        seq = jnp.concatenate([tok, seq], axis=1)
        seq = mamba_block(seq, in_proj_w, conv_w, conv_b, x_proj_w, dt_proj_w, dt_proj_b, A_log, D, out_proj_w)
        seq = seq[:, -H * W * R * R:, :]
        out = seq.reshape(B, H * R, W * R, D_MODEL).transpose(0, 3, 1, 2)
        return pixel_unshuffle(out, R)

    def _L0_ffn_ref(x, memory_tokens, memory_router):
        import jax, jax.numpy as jnp
        import numpy as np
        TOP_K = 8
        M, T, D = memory_tokens.shape
        x0 = x[:, 0, :]
        router_scores = x0 @ memory_router
        top_vals, top_idx = jax.lax.top_k(router_scores, TOP_K)
        router_weights = jax.nn.softmax(top_vals, axis=1)
        gathered = memory_tokens[top_idx]
        combined = jnp.einsum('bk,bktd->btd', router_weights, gathered)
        return x.at[:, 1:T + 1, :].set(combined)

    def _gn(v, G=32, eps=1e-05):
        B_, C_, H_, W_ = v.shape
        g = v.reshape(B_, G, C_ // G, H_, W_)
        m = jnp.mean(g, axis=(2, 3, 4), keepdims=True)
        s = jnp.var(g, axis=(2, 3, 4), keepdims=True)
        return ((g - m) / jnp.sqrt(s + eps)).reshape(v.shape)

    def _ln_c(v, eps=1e-06):
        m = jnp.mean(v, axis=1, keepdims=True)
        s = jnp.var(v, axis=1, keepdims=True)
        return (v - m) / jnp.sqrt(s + eps)

    def _ln_t(v, eps=1e-05):
        m = jnp.mean(v, axis=-1, keepdims=True)
        s = jnp.var(v, axis=-1, keepdims=True)
        return (v - m) / jnp.sqrt(s + eps)

    def _to_tokens(v):
        B_, C_, H_, W_ = v.shape
        return v.reshape(B_, C_, H_ * W_).transpose(0, 2, 1)

    def _from_tokens(t, like):
        B_, C_, H_, W_ = like.shape
        return t.transpose(0, 2, 1).reshape(B_, C_, H_, W_)
    x = x + _L0_conv_ref(_ln_c(x), L0_conv_global_token, L0_conv_in_proj_w, L0_conv_conv_w, L0_conv_conv_b, L0_conv_x_proj_w, L0_conv_dt_proj_w, L0_conv_dt_proj_b, L0_conv_A_log, L0_conv_D, L0_conv_out_proj_w)
    t = _to_tokens(x)
    t = t + _L0_ffn_ref(_ln_t(t), L0_ffn_memory_tokens, L0_ffn_memory_router)
    x = _from_tokens(t, x)
    return x

_drawn_inputs = setup_inputs


def setup_inputs(seed=0):
    import zlib

    import numpy as np

    out = dict(_drawn_inputs(seed))
    spreads = {'L0_conv_global_token': (0.0, 2.0), 'L0_conv_conv_b': (0.0, 0.8), 'L0_conv_D': (1.0, 0.6)}
    factors = {'L0_conv_in_proj_w': 8.0,
     'L0_conv_conv_w': 8.0,
     'L0_conv_x_proj_w': 8.0,
     'L0_conv_dt_proj_w': 8.0,
     'L0_conv_dt_proj_b': 8.0,
     'L0_conv_A_log': 8.0,
     'L0_conv_out_proj_w': 8.0,
     'L0_ffn_memory_tokens': 64.0,
     'L0_ffn_memory_router': 64.0}
    for name, (base, spread) in spreads.items():
        noise = np.random.default_rng([zlib.crc32(name.encode()), seed]).standard_normal(out[name].shape)
        drawn = base * np.exp(spread * noise) if base else spread * noise
        out[name] = jnp.asarray(drawn.astype(out[name].dtype))
    for name, factor in factors.items():
        out[name] = (out[name] * factor).astype(out[name].dtype)
    return out
```

```python
from contextlib import ExitStack

import concourse.bass as bass
from concourse import mybir
from concourse.bass import ds

F32 = mybir.dt.float32
BF16 = mybir.dt.bfloat16
U32 = mybir.dt.uint32
ACT = mybir.ActivationFunctionType
ALU = mybir.AluOpType

P = 128
BATCH, DIM, HH, WW = 4, 512, 24, 24
Q = DIM // P
HALVES = 2
NS = 16
RANK = 8
TAPS = 4
HIST = TAPS - 1
ROWS = 4
CHUNKS = HH // ROWS
TOK = ROWS * WW
T = TOK * Q
UNITS = CHUNKS * BATCH
SLOT = HIST + T
TOPK = 8
MEM, MT = 256, 128
BC = 2 * NS
PARTS = 3
DTROW = PARTS * BC
XROWS = DTROW + RANK
XP_M = XROWS
NEG_LIMIT = -44.0
EPS_C, EPS_T = 1e-6, 1e-5
LOG_C, LOG_D, LOG_G, LOG_H = 0.34222454, 1.83313539, 0.33814541, 1.75319741 ** 2
POOL_STATES = (5, 7, 9, 11, 13, 15)
NPOOL = len(POOL_STATES)
NDVE = NS - NPOOL
HRING, MRING, CRING = 8, 4, 4
LAG = 3
GRP = 4

STAGES_PER_UNIT = NS + NPOOL


def dve_index(n):
    return sum(1 for m in range(n) if m not in POOL_STATES)


def pool_index(n):
    return POOL_STATES.index(n)


def staged(s):
    return [("C", (s + 1) % NS)], [("B", s + 3)] * (s + 3 in POOL_STATES)


def stage_index(kind, n):
    order = [("C", 0)] + [it for s in range(NS - 1) for part in staged(s) for it in part]
    return order.index((kind, n))


def build(nc, x, tok, w_in, conv_w, conv_b, xp_w, dt_w, dt_b, a_log, dvec, op_w, mem, router, out):
    ctx = ExitStack()
    with ctx:
        def sb(name, shape, dt=F32):
            return ctx.enter_context(nc.sbuf_tensor(name, shape, dt))

        def sem(name):
            return ctx.enter_context(nc.semaphore(name))

        X = sb("X", [P, UNITS * T])
        XN = sb("XN", [P, (UNITS + BATCH) * SLOT])
        CAR = sb("CAR", [P, (UNITS + BATCH) * NS * HALVES])
        SCAN = sb("SCAN", [P, (HRING + MRING) * HALVES * T])
        HB = SCAN[:, 0:HRING * HALVES * T].rearrange("p (r h t) -> p r h t", r=HRING, h=HALVES)
        M = SCAN[:, HRING * HALVES * T:].rearrange("p (r h t) -> p r h t", r=MRING, h=HALVES)
        UDT = sb("UDT", [P, 6 * HALVES * T])
        UDTv = UDT[:, :].rearrange("p (k r h t) -> p k r h t", k=3, r=2, h=HALVES)
        U, DT, DTU = (UDTv[:, k] for k in range(3))
        CS = sb("CS", [P, CRING, T])
        BS = sb("BS", [P, 2, T])
        XC = sb("XC", [P, Q, TOK]); SQ = sb("SQ", [P, Q, TOK])
        LNV = sb("LNV", [P, TOK]); RSTD = sb("RSTD", [P, TOK])
        XC2 = sb("XC2", [P, Q, TOK]); SQ2 = sb("SQ2", [P, Q, TOK])
        LNV2 = sb("LNV2", [P, TOK]); RSTD2 = sb("RSTD2", [P, TOK])
        SG = sb("SG", [P, HALVES, T])
        SGZ = sb("SGZ", [P, HALVES, T])
        SE = sb("SE", [P, HALVES, T])
        SR = sb("SR", [P, HALVES, T])
        SS = sb("SS", [P, HALVES, T])
        GZ = sb("GZ", [P, HALVES, T])
        VV = sb("VV", [P, HALVES, T])
        PT = sb("PT", [DTROW, 2, T], BF16)
        PART = sb("PART", [DTROW, T], BF16)
        LESS = sb("LESS", [DTROW, PARTS - 1])
        XDT = sb("XDT", [P, T])
        WT = sb("WT", [P, HALVES, TAPS, P])
        WZT = sb("WZT", [P, HALVES, P])
        XPT = sb("XPT", [P, HALVES, XP_M])
        DTW = sb("DTW", [P, HALVES, P])
        OPT = sb("OPT", [P, HALVES, P])
        IDENT = sb("IDENT", [P, P]); MEANW = sb("MEANW", [P, P])
        SEL = sb("SEL", [DTROW, BC, P], BF16)
        A = sb("A", [P, HALVES, NS]); AE = sb("AE", [P, HALVES, NS])
        CB_ = sb("conv_bias", [P, HALVES]); DV = sb("DV", [P, HALVES])
        CW = sb("CW", [P, HALVES, TAPS])
        EPSC = sb("EPSC", [P, 1]); EPST = sb("EPST", [P, 1])
        LOGB = sb("LOGB", [P, 2])
        RW = sb("RW", [P, Q, MEM])
        WNAT = SCAN[:, 0:512].rearrange("p (k c) -> p k c", k=4)
        WSC = SCAN[:, 512:1536].rearrange("p (k c) -> p k c", k=8)
        OPNAT = SCAN[:, 1536:1792]
        XPNAT = SCAN[0:RANK + BC, 1792:2048]
        DTNAT = SCAN[:, 2048:2048 + 2 * (XROWS + 1)].rearrange("p (k c) -> p k c", k=2)
        TKC = SCAN[:, 2304:2305]
        TU = SCAN[:, 2306:2308]; TSG = SCAN[:, 2308:2310]; TUC = SCAN[:, 2310:2312]
        TL = SCAN[:, 2312:2314]; TR = SCAN[:, 2576:2578]; TS = SCAN[:, 2578:2580]; TDT = SCAN[:, 2314:2316]; TDU = SCAN[:, 2316:2318]
        UB = SCAN[:, 2320:2576].rearrange("p (k c) -> p k c", k=2)
        GR = 16
        G = SCAN[:, 0:GR * DIM].rearrange("p (r d) -> p r d", r=GR)
        WI = UDT[:, 0:BATCH * TOPK * P].rearrange("p (k t) -> p k t", t=P)
        x0 = SCAN[:, GR * DIM:GR * DIM + 16].rearrange("p (q b) -> p q b", q=Q)
        x0s = SCAN[:, GR * DIM + 16:GR * DIM + 32].rearrange("p (q b) -> p q b", q=Q)
        r0 = SCAN[:, GR * DIM + 32:GR * DIM + 36]
        SCO = SCAN[0:BATCH, GR * DIM + 64:GR * DIM + 64 + MEM]
        TOP = SCAN[0:BATCH, GR * DIM + 320:GR * DIM + 328]
        NMX = SCAN[0:BATCH, GR * DIM + 328:GR * DIM + 329]
        WEX = SCAN[0:BATCH, GR * DIM + 336:GR * DIM + 344]
        WSUM = SCAN[0:BATCH, GR * DIM + 344:GR * DIM + 345]
        WRC = SCAN[0:BATCH, GR * DIM + 345:GR * DIM + 346]
        WNM = SCAN[0:BATCH, GR * DIM + 352:GR * DIM + 360]
        WDG = SCAN[0:BATCH, GR * DIM + 360:GR * DIM + 392].rearrange("p (b k) -> p b k", b=BATCH)
        WBC = SCAN[:, GR * DIM + 400:GR * DIM + 432]
        IDX = sb("IDX", [BATCH, TOPK], U32)
        ONE4 = sb("ONE4", [BATCH, P])

        Yp = ctx.enter_context(nc.psum_tensor("Yp", [P, HALVES, 512], F32))
        DA = ctx.enter_context(nc.psum_tensor("DA", [P, HALVES, 512], F32))
        BB = ctx.enter_context(nc.psum_tensor("BB", [P, 512], F32))
        ST = ctx.enter_context(nc.psum_tensor("ST", [P, 512], F32))
        PP = ctx.enter_context(nc.psum_tensor("PP", [P, HALVES, 512], F32))
        STAT = BB[:, 0:TOK]
        PPT = PP[:, :, 0:T]

        w_loaded = sem("w_loaded"); x0_loaded = sem("x0_loaded"); x_loaded = sem("x_loaded")
        ffn_loaded = sem("ffn_loaded")
        const_ready = sem("const_ready")
        zeroed = sem("zeroed")
        less_set = sem("less_set")
        set_pe = sem("set_pe"); set_act = sem("set_act"); set_dve = sem("set_dve")
        mean_ready = sem("mean_ready"); xc_ready = sem("xc_ready"); sq_ready = sem("sq_ready")
        var_ready = sem("var_ready"); ln_done = sem("ln_done"); rstd_ready = sem("rstd_ready")
        xn_part = sem("xn_part"); xn_ready = sem("xn_ready")
        conv_ready = sem("conv_ready"); clamped = sem("clamped"); sg_chain = sem("sg_chain")
        sg_ready = sem("sg_ready"); u_ready = sem("u_ready"); xp_ready = sem("xp_ready")
        hi_ready = sem("hi_ready"); res_ready = sem("res_ready"); mid_ready = sem("mid_ready")
        parts_ready = sem("parts_ready"); dtp_ready = sem("dtp_ready"); sp_chain = sem("sp_chain")
        sq_e_ready = sem("sq_e_ready"); cr_ready = sem("cr_ready"); r2_ready = sem("r2_ready"); m1_done = sem("m1_done"); dt_ready = sem("dt_ready"); dtu_ready = sem("dtu_ready")
        b_ready = sem("b_ready"); dbu_dve = sem("dbu_dve"); dbu_pool = sem("dbu_pool")
        st_ready = sem("st_ready"); st_copied = sem("st_copied")
        da_ready = sem("da_ready"); scan_done = sem("scan_done"); car_saved = sem("car_saved")
        m_ready = sem("m_ready"); ysum_done = sem("ysum_done")
        z_ready = sem("z_ready"); z_clamped = sem("z_clamped"); sgz_chain = sem("sgz_chain")
        sgz_ready = sem("sgz_ready"); gz_ready = sem("gz_ready"); v_ready = sem("v_ready")
        vg_ready = sem("vg_ready"); op_ready = sem("op_ready"); x2_ready = sem("x2_ready")
        mean2_ready = sem("mean2_ready"); xc2_ready = sem("xc2_ready"); sq2_ready = sem("sq2_ready")
        var2_ready = sem("var2_ready"); ln2_done = sem("ln2_done"); rstd2_ready = sem("rstd2_ready")
        xh2_done = sem("xh2_done"); out_ready = sem("out_ready"); stored = sem("stored")
        f_pe = sem("f_pe"); f_act = sem("f_act"); f_dve = sem("f_dve")
        idx_ready = sem("idx_ready"); g_loaded = [sem(f"g_loaded{b}") for b in range(BATCH)]
        g_used = sem("g_used"); comb_done = sem("comb_done")

        N_WLOADS = 11
        block = ctx.enter_context(nc.Block())

        def unit_x(j):
            return X[:, ds(j * T, T)].rearrange("p (q t) -> p q t", q=Q)

        def unit_seq(j):
            return XN[:, ds(j * SLOT + HIST, T)]

        def by_row_parity(ap_qt, r1):
            return ap_qt[:, 2 * r1:2 * r1 + 2, :].rearrange("p r (h w) -> p h w r", w=WW)

        def seq_rows(ap_t, r1):
            return ap_t.rearrange("p (h r w s) -> p h r w s", h=ROWS, r=2, w=WW)[:, :, r1]

        def over_q(ap):
            return ap.unsqueeze(1).broadcast_to([P, Q, TOK])

        def over_halves(ap):
            return ap.unsqueeze(1).broadcast_to([P, HALVES, T])

        def positive(eng, s, v):
            if isinstance(v, int) and v <= 0:
                return
            assert isinstance(v, int) or v.min_val > 0
            eng.wait_ge(s, v)

        def run_units(eng, step, first_main=None):
            def unit(J, par, main=True, front=True, back=True, norm=True):
                prev = back
                for s in range(NS):
                    step(J, par, s, main, front, back, prev, norm)
            unit(-2, 0, main=False, front=False, back=False)
            unit(-1, 1, main=False, back=False)
            if first_main:
                first_main()
            unit(0, 0, back=False)
            unit(1, 1)
            with eng.Fori(1, (UNITS - 2) // 2) as i:
                unit(2 * i, 0)
                unit(2 * i + 1, 1)
            unit(UNITS - 2, 0, norm=False)
            unit(UNITS - 1, 1, front=False, norm=False)
            unit(UNITS, 0, main=False, front=False, norm=False)

        @block.sync
        def _(sp):
            xv = x.rearrange("b (p q) (c s) w -> c p b q (s w)", q=Q, s=ROWS)
            ov = out.rearrange("b (p q) (c s) w -> c b p q (s w)", q=Q, s=ROWS)
            Xc = X[:, :].rearrange("p (c b q t) -> p c b q t", c=CHUNKS, b=BATCH, q=Q)
            sp.dma_start(WNAT, w_in.rearrange("(k e) c -> e k c", e=P)).then_inc(w_loaded, 16)
            sp.dma_start(Xc[:, 0, 0], xv[0, :, 0]).then_inc(x0_loaded, 16)
            sp.dma_start(CW[:, :, :], conv_w.rearrange("(k e) t -> e k t", e=P)).then_inc(w_loaded, 16)
            sp.dma_start(OPNAT, op_w).then_inc(w_loaded, 16)
            sp.dma_start(XPNAT, xp_w).then_inc(w_loaded, 16)
            sp.dma_start(CB_[:, :], conv_b.rearrange("(k e) -> e k", e=P), allow_slow_non_contiguous=True).then_inc(w_loaded, 16)
            sp.dma_start(DV[:, :], dvec.rearrange("(k e) -> e k", e=P), allow_slow_non_contiguous=True).then_inc(w_loaded, 16)
            sp.dma_start(AE[:, :, :], a_log.rearrange("(k e) n -> e k n", e=P)).then_inc(w_loaded, 16)
            sp.dma_start(TKC, tok.rearrange("a b c -> c (a b)"), allow_slow_non_contiguous=True).then_inc(w_loaded, 16)
            sp.wait_ge(zeroed, 1)
            sp.dma_start(DTNAT[:, :, DTROW:XROWS],
                         dt_w.rearrange("(k e) r -> e k r", e=P)).then_inc(w_loaded, 16)
            sp.dma_start(DTNAT[:, :, XROWS:XROWS + 1],
                         dt_b.rearrange("(k e r) -> e k r", e=P, r=1), allow_slow_non_contiguous=True).then_inc(w_loaded, 16)
            sp.dma_start(RW[:, :, :], router.rearrange("(p q) m -> p q m", q=Q)).then_inc(w_loaded, 16)
            for b in range(1, BATCH):
                sp.dma_start(Xc[:, 0, b], xv[0, :, b]).then_inc(x_loaded, 16)
            for c in range(1, CHUNKS):
                for b in range(BATCH):
                    sp.dma_start(Xc[:, c, b], xv[c, :, b]).then_inc(x_loaded, 16)

            def store(c, b, j):
                sp.wait_ge(out_ready, j + 1)
                sp.dma_start(ov[ds(c, 1), ds(b, 1)].rearrange("c b p q t -> (c b p) q t"),
                             unit_seq(j).rearrange("p (q t) -> p q t", q=Q)).then_inc(stored, 16)
            with sp.Fori(2, CHUNKS) as c:
                with sp.Fori(0, BATCH) as b:
                    store(c, b, c * BATCH + b)

            sp.wait_ge(idx_ready, 1)
            sp.wait_ge(ysum_done, NS * UNITS)
            for b in range(BATCH):
                if b >= 2:
                    sp.wait_ge(g_used, b - 1)
                for k in range(TOPK):
                    m = sp.value_load(IDX[b:b + 1, k:k + 1], min_val=0, max_val=MEM - 1)
                    sp.dma_start(G[:, (b % 2) * TOPK + k, :],
                                 mem[ds(m, 1)].rearrange("a t d -> (a t) d")).then_inc(g_loaded[b], 16)
            sp.wait_ge(comb_done, BATCH)
            for c in range(2):
                for b in range(BATCH):
                    sp.dma_start(ov[c, b], unit_seq(c * BATCH + b).rearrange("p (q t) -> p q t", q=Q))\
                        .then_inc(stored, 16)
            sp.wait_ge(stored, 16 * UNITS)

        @block.gpsimd
        def _(pool):
            pool.memset(DTNAT, 0.0).then_inc(zeroed, 1)
            pool.memset(IDENT[:, :], 0.0).then_inc(zeroed, 1)
            pool.memset(SEL[:, :, :], 0.0).then_inc(zeroed, 1)
            pool.memset(MEANW[:, :], 1.0 / DIM).then_inc(const_ready, 1)
            pool.memset(XDT[:, :], 1.0).then_inc(const_ready, 1)
            pool.memset(EPSC[:, :], EPS_C).then_inc(const_ready, 1)
            pool.memset(EPST[:, :], EPS_T).then_inc(const_ready, 1)
            pool.memset(LOGB[:, 0:1], 2.0 / LOG_C).then_inc(const_ready, 1)
            pool.memset(LOGB[:, 1:2], -LOG_G).then_inc(const_ready, 1)
            pool.memset(ONE4[:, :], 1.0).then_inc(const_ready, 1)
            for b in range(BATCH):
                pool.memset(XN[:, b * SLOT:b * SLOT + HIST - 1], 0.0).then_inc(const_ready, 1)
            pool.wait_ge(zeroed, 3)
            pool.affine_select(out=IDENT[:, :], in_=IDENT[:, :], compare_op=ALU.not_equal, fill=1.0,
                               base=0, pattern=[[-1, P]], channel_multiplier=1).then_inc(const_ready, 1)
            for part in range(PARTS):
                if part:
                    pool.wait_ge(zeroed, 3 + part)
                pool.affine_select(out=SEL[:, :, :], in_=SEL[:, :, :], compare_op=ALU.not_equal, fill=1.0,
                                   base=-part * BC, pattern=[[-1, BC], [0, P]],
                                   channel_multiplier=1).then_inc(zeroed if part < PARTS - 1 else const_ready, 1)
            pool.wait_ge(w_loaded, 16 * N_WLOADS)
            for b in range(BATCH):
                pool.tensor_copy(XN[:, b * SLOT + HIST - 1:b * SLOT + HIST], TKC).then_inc(const_ready, 1)

            def step(J, par, s, main, front, back, prev, norm):
                f, k, g, N = J + 1, J - 1, J + 2, NS * J + s
                fp = kp = 1 - par
                if main and (s > 0 or prev) or (s == 0 and prev):
                    n1 = (s - 1) % NS
                    unit1 = J if s else J - 1
                    pool.wait_ge(scan_done, 2 * N)
                    pool.wait_ge(st_copied, STAGES_PER_UNIT * unit1 + stage_index("C", n1) + 1)
                    positive(pool, ysum_done, N - MRING)
                    pool.tensor_tensor(M[:, n1 % MRING], HB[:, n1 % HRING],
                                       over_halves(CS[:, n1 % CRING]), ALU.mult).then_inc(m_ready, 1)
                if main and s + 2 in POOL_STATES:
                    n2 = s + 2
                    pool.wait_ge(st_copied, STAGES_PER_UNIT * J + stage_index("B", n2) + 1)
                    pool.wait_ge(dtu_ready, J + 1)
                    pool.wait_ge(car_saved, 4 * BATCH + 4 * J + (n2 - HRING) // GRP + 1)
                    pool.tensor_tensor(HB[:, n2 % HRING], DTU[:, par], over_halves(BS[:, pool_index(n2) % 2]),
                                       ALU.mult).then_inc(dbu_pool, 1)
                if back and s == 4:
                    pool.wait_ge(gz_ready, k + 1)
                    pool.wait_ge(v_ready, k + 1)
                    pool.tensor_tensor(VV[:, :, :], VV[:, :, :], GZ[:, :, :], ALU.mult).then_inc(vg_ready, 1)
                if front and s == 10:
                    pool.wait_ge(sq_e_ready, f + 1)
                    pool.tensor_tensor(SE[:, :, :], SE[:, :, :], SR[:, :, :], ALU.mult).then_inc(cr_ready, 1)
                if back and s == 12:
                    pool.wait_ge(rstd2_ready, k + 1)
                    pool.tensor_tensor(XC2[:, :, :], XC2[:, :, :], over_q(RSTD2[:, :]), ALU.mult)\
                        .then_inc(xh2_done, 1)
                if back and s == 13:
                    pool.wait_ge(xh2_done, k + 1)
                    pool.tensor_tensor(unit_seq(k).rearrange("p (q t) -> p q t", q=Q), XC2[:, :, :], unit_x(k),
                                       ALU.add).then_inc(out_ready, 1)
                if front and s == 13:
                    pool.wait_ge(dt_ready, f + 1)
                    pool.tensor_tensor(DTU[:, fp], DT[:, fp], U[:, fp], ALU.mult).then_inc(dtu_ready, 1)
                if norm and s == 6:
                    pool.wait_ge(rstd_ready, g + 1)
                    for r1 in range(2):
                        pool.tensor_tensor(seq_rows(unit_seq(g), r1), by_row_parity(XC[:, :, :], r1),
                                           by_row_parity(over_q(RSTD[:, :]), r1), ALU.mult).then_inc(xn_part, 1)
                    pool.wait_ge(xn_part, 2 * (g + 1))
                    pool.tensor_copy(XN[:, ds((g + BATCH) * SLOT, HIST)],
                                     XN[:, ds(g * SLOT + T, HIST)]).then_inc(xn_ready, 1)

            run_units(pool, step)

        @block.scalar
        def _(act):
            act.preload_act_table_set("natural_log_exp_and_others")
            act.wait_ge(w_loaded, 16 * N_WLOADS)
            act.wait_ge(const_ready, 7)
            act.activation(A[:, :, :], AE[:, :, :], ACT.Exp).then_inc(set_act, 1)
            act.wait_ge(set_act, 1)
            act.activation(A[:, :, :], A[:, :, :], ACT.Copy, scale=-1.0).then_inc(set_act, 1)
            act.wait_ge(set_pe, 1)
            act.activation(WT[:, :, :, :].rearrange("p h k c -> p h (k c)"), Yp[:, :, :], ACT.Copy)\
                .then_inc(set_act, 1)
            act.wait_ge(set_pe, 2)
            act.activation(WZT[:, :, :].rearrange("p h c -> p (h c)"), PP[:, 0, 0:256], ACT.Copy)
            act.activation(OPT[:, :, :].rearrange("p h c -> p (h c)"), PP[:, 0, 256:512], ACT.Copy)
            for h in range(HALVES):
                xp = PP[:, 1, h * 40:h * 40 + 40]
                for part in range(PARTS):
                    act.activation(XPT[:, h, part * BC:(part + 1) * BC], xp[:, RANK:RANK + BC], ACT.Copy)
                act.activation(XPT[:, h, DTROW:XROWS], xp[:, 0:RANK], ACT.Copy)
                last = act.activation(DTW[DTROW:XROWS + 1, h], PP[DTROW:XROWS + 1, 1, 128 + h * P:256 + h * P],
                                      ACT.Copy)
            last.then_inc(set_act, 1)
            act.wait_ge(set_dve, 3)
            act.activation(TSG, TUC, ACT.Exp, scale=-1.0).then_inc(set_act, 1)
            act.wait_ge(set_act, 5)
            act.activation(TSG, TSG, ACT.Ln, bias=1.0).then_inc(set_act, 1)
            act.wait_ge(set_act, 6)
            act.activation(TSG, TSG, ACT.Exp, scale=-1.0).then_inc(set_act, 1)
            act.wait_ge(set_pe, 4)
            act.activation(XDT[DTROW:XROWS, 0:1], DA[DTROW:XROWS, 0, 8:9], ACT.Copy).then_inc(set_act, 1)
            act.wait_ge(set_pe, 5)
            act.activation(TL, DA[:, 0, 40:42], ACT.Abs).then_inc(set_act, 1)
            act.wait_ge(set_act, 9)
            act.activation(TL, TL, ACT.Exp, scale=-1.0).then_inc(set_act, 1)
            act.wait_ge(set_act, 10)
            act.activation(TR, TL, ACT.Ln, bias=LOGB[:, 0:1], scale=1.0 / LOG_C).then_inc(set_act, 1)
            act.wait_ge(set_act, 11)
            act.activation(TR, TR, ACT.Exp, scale=-1.0).then_inc(set_act, 1)
            act.wait_ge(set_dve, 6)
            act.activation(TR, TL, ACT.Square, scale=1.0 / LOG_C).then_inc(set_act, 1)
            act.wait_ge(set_act, 13)
            act.activation(TS, TR, ACT.Square, bias=LOGB[:, 1:2]).then_inc(set_act, 1)

            def decay(J, par, n, N, h):
                positive(act, scan_done, 2 * N - 1 + h)
                act.activation(DA[:, h, 0:T], DT[:, par, h], ACT.Exp, scale=A[:, h, n:n + 1])\
                    .then_inc(da_ready, 1)

            def step(J, par, s, main, front, back, prev, norm):
                f, k, g, N = J + 1, J - 1, J + 2, NS * J + s
                fp = kp = 1 - par
                if main:
                    if s < NS - 1:
                        unit, upar, n1 = J, par, s + 1
                    else:
                        unit, upar, n1 = J + 1, 1 - par, 0
                    if s < NS - 1 or front:
                        if n1 == 0:
                            act.wait_ge(dt_ready, unit + 1)
                        decay(unit, upar, n1, N + 1, 0)
                        act.wait_ge(st_ready, STAGES_PER_UNIT * unit + stage_index("C", n1) + 1)
                        positive(act, m_ready, N + 2 - CRING)
                        act.activation(CS[:, n1 % CRING], ST[:, 0:T], ACT.Copy).then_inc(st_copied, 1)
                        decay(unit, upar, n1, N + 1, 1)
                    for _, n in staged(s)[1]:
                        act.wait_ge(st_ready, STAGES_PER_UNIT * J + stage_index("B", n) + 1)
                        positive(act, dbu_pool, NPOOL * J + pool_index(n) - 1)
                        act.activation(BS[:, pool_index(n) % 2], ST[:, 0:T], ACT.Copy).then_inc(st_copied, 1)
                if front and s == 4:
                    act.wait_ge(clamped, 2 * f + 2)
                    positive(act, u_ready, f)
                    act.activation(SG[:, :, :], PPT, ACT.Exp, scale=-1.0).then_inc(sg_chain, 1)
                    act.wait_ge(sg_chain, 2 * f + 1)
                    act.activation(SG[:, :, :], SG[:, :, :], ACT.Ln, bias=1.0).then_inc(sg_chain, 1)
                    act.wait_ge(sg_chain, 2 * f + 2)
                    act.activation(SG[:, :, :], SG[:, :, :], ACT.Exp, scale=-1.0).then_inc(sg_ready, 1)
                if front and s == 6:
                    act.wait_ge(xp_ready, f + 1)
                    positive(act, parts_ready, f)
                    act.activation(PART[:, :], PP[0:DTROW, 1, 0:T], ACT.Copy)
                    act.activation(XDT[DTROW:XROWS, :], PP[DTROW:XROWS, 1, 0:T], ACT.Copy).then_inc(hi_ready, 1)
                if front and s == 7:
                    act.wait_ge(res_ready, f + 1)
                    act.activation(PART[:, :], PP[0:DTROW, 1, 0:T], ACT.Copy).then_inc(mid_ready, 1)
                if back and s == 10:
                    act.wait_ge(xc2_ready, k + 1)
                    act.activation(SQ2[:, :, :], XC2[:, :, :], ACT.Square).then_inc(sq2_ready, 1)
                if back and s == 11:
                    act.wait_ge(var2_ready, k + 1)
                    act.activation(LNV2[:, :], STAT, ACT.Ln, bias=EPST[:, 0:1]).then_inc(ln2_done, 1)
                    act.wait_ge(ln2_done, k + 1)
                    positive(act, out_ready, k)
                    act.activation(RSTD2[:, :], LNV2[:, :], ACT.Exp, scale=-0.5).then_inc(rstd2_ready, 1)
                if front and s == 9:
                    act.wait_ge(dtp_ready, f + 1)
                    positive(act, dt_ready, f)
                    act.activation(SE[:, :, :], PPT, ACT.Abs).then_inc(sp_chain, 1)
                    act.wait_ge(sp_chain, 3 * f + 1)
                    act.activation(SE[:, :, :], SE[:, :, :], ACT.Exp, scale=-1.0).then_inc(sp_chain, 1)
                    act.wait_ge(sp_chain, 3 * f + 2)
                    act.activation(SR[:, :, :], SE[:, :, :], ACT.Ln, bias=LOGB[:, 0:1], scale=1.0 / LOG_C)\
                        .then_inc(sp_chain, 1)
                    act.wait_ge(sp_chain, 3 * f + 3)
                    act.activation(SR[:, :, :], SR[:, :, :], ACT.Exp, scale=-1.0).then_inc(sq_e_ready, 1)
                if front and s == 11:
                    act.wait_ge(cr_ready, f + 1)
                    act.activation(SR[:, :, :], SE[:, :, :], ACT.Square, scale=1.0 / LOG_C).then_inc(r2_ready, 1)
                    act.wait_ge(r2_ready, 2 * f + 1)
                    act.activation(SS[:, :, :], SR[:, :, :], ACT.Square, bias=LOGB[:, 1:2]).then_inc(r2_ready, 1)
                if norm and s == 4:
                    act.wait_ge(xc_ready, g + 1)
                    positive(act, var_ready, g)
                    act.activation(SQ[:, :, :], XC[:, :, :], ACT.Square).then_inc(sq_ready, 1)
                if norm and s == 5:
                    act.wait_ge(var_ready, g + 1)
                    act.activation(LNV[:, :], STAT, ACT.Ln, bias=EPSC[:, 0:1]).then_inc(ln_done, 1)
                    act.wait_ge(ln_done, g + 1)
                    positive(act, xn_ready, g)
                    act.activation(RSTD[:, :], LNV[:, :], ACT.Exp, scale=-0.5).then_inc(rstd_ready, 1)
                if main and s == 14:
                    act.wait_ge(z_clamped, J + 1)
                    positive(act, gz_ready, J)
                    act.activation(SGZ[:, :, :], PPT, ACT.Exp, scale=-1.0).then_inc(sgz_chain, 1)
                    act.wait_ge(sgz_chain, 2 * J + 1)
                    act.activation(SGZ[:, :, :], SGZ[:, :, :], ACT.Ln, bias=1.0).then_inc(sgz_chain, 1)
                    act.wait_ge(sgz_chain, 2 * J + 2)
                    act.activation(SGZ[:, :, :], SGZ[:, :, :], ACT.Exp, scale=-1.0).then_inc(sgz_ready, 1)

            def first_main():
                act.wait_ge(dt_ready, 1)
                decay(0, 0, 0, 0, 0)
                act.wait_ge(st_ready, 1)
                act.activation(CS[:, 0], ST[:, 0:T], ACT.Copy).then_inc(st_copied, 1)
                decay(0, 0, 0, 0, 1)

            run_units(act, step, first_main)

            act.wait_ge(f_dve, 1)
            act.activation(x0s, x0, ACT.Square).then_inc(f_act, 1)
            act.wait_ge(f_pe, 2)
            act.activation(r0, PP[:, 0, 4:8], ACT.Ln, bias=EPST[:, 0:1]).then_inc(f_act, 1)
            act.wait_ge(f_act, 2)
            act.activation(r0, r0, ACT.Exp, scale=-0.5).then_inc(f_act, 1)
            act.wait_ge(f_dve, 5)
            act.activation(WEX, TOP, ACT.Exp, bias=NMX, accum_out=WSUM).then_inc(f_act, 1)

        @block.tensor
        def _(pe):
            pe.wait_ge(const_ready, 7 + BATCH + 2)
            pe.wait_ge(w_loaded, 16 * N_WLOADS)
            pe.wait_ge(set_dve, 1)
            for h in range(HALVES):
                for k in range(TAPS):
                    last = pe.transpose(Yp[:, h, k * P:(k + 1) * P], WSC[:, h * TAPS + k], IDENT[:, :])
            last.then_inc(set_pe, 1)
            for h in range(HALVES):
                pe.transpose(PP[:, 0, h * P:(h + 1) * P], WNAT[:, HALVES + h], IDENT[:, :])
                pe.transpose(PP[:, 0, 256 + h * P:256 + (h + 1) * P], OPNAT[:, h * P:(h + 1) * P], IDENT[:, :])
                pe.transpose(PP[:, 1, h * 40:h * 40 + 40], XPNAT[:, h * P:(h + 1) * P], IDENT[0:40, 0:40])
                last = pe.transpose(PP[0:XROWS + 1, 1, 128 + h * P:256 + h * P], DTNAT[:, h], IDENT[:, :])
            last.then_inc(set_pe, 1)
            pe.wait_ge(set_act, 4)
            for h in range(HALVES):
                last = pe.matmul(DA[:, 0, h:h + 1], WT[:, h, TAPS - 1], TKC, start=True, stop=True)
            last.then_inc(set_pe, 1)
            pe.wait_ge(set_dve, 5)
            for h in range(HALVES):
                pe.matmul(DA[0:XROWS, 0, 8:9], XPT[:, h, :], TU[:, h:h + 1], start=h == 0, stop=h == 1)
            for h in range(HALVES):
                last = pe.matmul(DA[:, 0, 16:32], UB[:, h], XPT[:, h, 0:NS], start=h == 0, stop=h == 1)
            last.then_inc(set_pe, 1)
            pe.wait_ge(set_act, 8)
            for h in range(HALVES):
                last = pe.matmul(DA[:, 0, 40 + h:41 + h], DTW[DTROW:XROWS + 1, h], XDT[DTROW:XROWS + 1, 0:1],
                                 start=True, stop=True, tile_position=(DTROW, 0))
            last.then_inc(set_pe, 1)

            def spread_b(unit, par, n):
                before = NDVE * unit + dve_index(n)
                positive(pe, dbu_dve, before)
                pe.matmul(BB[:, 0:T], SEL[:, n], PT[:, par], start=True, stop=True).then_inc(b_ready, 1)

            def spread_c(unit, par, n):
                positive(pe, st_copied, STAGES_PER_UNIT * unit + stage_index("C", n))
                pe.matmul(ST[:, 0:T], SEL[:, NS + n], PT[:, par], start=True, stop=True).then_inc(st_ready, 1)

            def step(J, par, s, main, front, back, prev, norm):
                f, k, g, N = J + 1, J - 1, J + 2, NS * J + s
                fp = kp = 1 - par
                if main and (s < NS - 1 or front):
                    unit, upar = (J, par) if s < NS - 1 else (J + 1, 1 - par)
                    for _, n in staged(s)[0]:
                        spread_c(unit, upar, n)
                if main and s >= LAG or prev and s < LAG:
                    n3 = (s - LAG) % NS
                    pe.wait_ge(m_ready, N - LAG + 1)
                    if s == LAG:
                        positive(pe, v_ready, J)
                    for h in range(HALVES):
                        last = pe.matmul(Yp[:, h, 0:T], IDENT[:, :], M[:, n3 % MRING, h],
                                         start=n3 == 0, stop=n3 == NS - 1)
                    last.then_inc(ysum_done, 1)
                if main:
                    for _, n in staged(s)[1]:
                        pe.wait_ge(st_copied, STAGES_PER_UNIT * J + stage_index("B", n))
                        pe.matmul(ST[:, 0:T], SEL[:, n], PT[:, par], start=True, stop=True).then_inc(st_ready, 1)
                    if norm and s == 4:
                        pe.wait_ge(xc_ready, g + 1)
                    if norm and s == 6:
                        pe.wait_ge(ln_done, g + 1)
                    if back and s == 10:
                        pe.wait_ge(xc2_ready, k + 1)
                    if back and s == 12:
                        pe.wait_ge(ln2_done, k + 1)
                    if s + 2 < NS and s + 2 not in POOL_STATES:
                        spread_b(J, par, s + 2)
                    elif s + 2 >= NS and front:
                        spread_b(J + 1, 1 - par, s + 2 - NS)
                if front and s in (1, 2):
                    h = s - 1
                    if h == 0:
                        pe.wait_ge(xn_ready, f + 1)
                        if main:
                            positive(pe, gz_ready, k + 1)
                    for tap in range(TAPS):
                        last = pe.matmul(PP[:, h, 0:T], WT[:, h, tap], XN[:, ds(f * SLOT + tap, T)],
                                         start=tap == 0, stop=tap == TAPS - 1)
                    last.then_inc(conv_ready, 1)
                if front and s == 6:
                    pe.wait_ge(u_ready, f + 1)
                    for h in range(HALVES):
                        last = pe.matmul(PP[0:XROWS, 1, 0:T], XPT[:, h], U[:, fp, h], start=h == 0, stop=h == 1)
                    last.then_inc(xp_ready, 1)
                if back and s == 6:
                    pe.wait_ge(vg_ready, k + 1)
                    if front:
                        pe.wait_ge(u_ready, f + 1)
                    for h in range(HALVES):
                        last = pe.matmul(PP[:, 0, 0:T], OPT[:, h], VV[:, h], start=h == 0, stop=h == 1)
                    last.then_inc(op_ready, 1)
                if front and s == 9:
                    pe.wait_ge(hi_ready, f + 1)
                    pe.wait_ge(parts_ready, f + 1)
                    if back:
                        pe.wait_ge(x2_ready, k + 1)
                    for h in range(HALVES):
                        last = pe.matmul(PP[:, h, 0:T], DTW[DTROW:XROWS + 1, h], XDT[DTROW:XROWS + 1, :],
                                         start=True, stop=True, tile_position=(DTROW, 0))
                    last.then_inc(dtp_ready, 1)
                if main and (norm and s in (3, 5) or back and s in (9, 11)):
                    pe.wait_ge(dbu_dve, NDVE * J + dve_index(s + 2))
                if back and s == 9:
                    pe.wait_ge(x2_ready, k + 1)
                    for q in range(Q):
                        last = pe.matmul(STAT, MEANW[:, :], unit_x(k)[:, q], start=q == 0, stop=q == Q - 1)
                    last.then_inc(mean2_ready, 1)
                if back and s == 11:
                    pe.wait_ge(sq2_ready, k + 1)
                    for q in range(Q):
                        last = pe.matmul(STAT, MEANW[:, :], SQ2[:, q], start=q == 0, stop=q == Q - 1)
                    last.then_inc(var2_ready, 1)
                if norm and s == 3:
                    if isinstance(g, int) and g == 0:
                        pe.wait_ge(x0_loaded, 16)
                    else:
                        pe.wait_ge(x_loaded, 16 * (UNITS - 1))
                    positive(pe, ln_done, g)
                    for q in range(Q):
                        last = pe.matmul(STAT, MEANW[:, :], unit_x(g)[:, q], start=q == 0, stop=q == Q - 1)
                    last.then_inc(mean_ready, 1)
                if norm and s == 5:
                    pe.wait_ge(sq_ready, g + 1)
                    for q in range(Q):
                        last = pe.matmul(STAT, MEANW[:, :], SQ[:, q], start=q == 0, stop=q == Q - 1)
                    last.then_inc(var_ready, 1)
                if main and s == 13:
                    if front:
                        pe.wait_ge(dt_ready, f + 1)
                    else:
                        pe.wait_ge(x2_ready, k + 1)
                    for h in range(HALVES):
                        last = pe.matmul(PP[:, h, 0:T], WZT[:, h], unit_seq(J), start=True, stop=True)
                    last.then_inc(z_ready, 1)

            def first_main():
                pe.wait_ge(parts_ready, 1)
                pe.wait_ge(ln_done, 2)
                spread_b(0, 0, 0)
                spread_c(0, 0, 0)
                spread_b(0, 0, 1)

            run_units(pe, step, first_main)

            X0v = X[:, 0:BATCH * T].rearrange("p (b q t) -> p q b t", b=BATCH, q=Q)[:, :, :, 0]
            pe.wait_ge(out_ready, UNITS)
            for q in range(Q):
                last = pe.matmul(PP[:, 0, 0:4], MEANW[:, :], X0v[:, q], start=q == 0, stop=q == Q - 1)
            last.then_inc(f_pe, 1)
            pe.wait_ge(f_act, 1)
            for q in range(Q):
                last = pe.matmul(PP[:, 0, 4:8], MEANW[:, :], x0s[:, q], start=q == 0, stop=q == Q - 1)
            last.then_inc(f_pe, 1)
            pe.wait_ge(f_dve, 2)
            for q in range(Q):
                last = pe.matmul(PP[0:BATCH, 1, 0:MEM], x0[:, q], RW[:, q], start=q == 0, stop=q == Q - 1)
            last.then_inc(f_pe, 1)
            pe.wait_ge(f_dve, 8)
            pe.matmul(PP[:, 0, 16:48], ONE4[:, :], WDG.rearrange("p b k -> p (b k)"), start=True, stop=True)\
                .then_inc(f_pe, 1)
            pe.wait_ge(f_dve, 10)
            for b in range(BATCH):
                pe.wait_ge(g_loaded[b], 16 * TOPK)
                for q in range(Q):
                    for k in range(TOPK):
                        last = pe.matmul((Yp[:, b % 2] if b < 2 else DA[:, b % 2])[:, q * P:(q + 1) * P],
                                         G[:, (b % 2) * TOPK + k].rearrange("p (c q) -> p q c", q=Q)[:, q],
                                         WI[:, b * TOPK + k], start=k == 0, stop=k == TOPK - 1)
                last.then_inc(g_used, 1)

        @block.vector
        def _(dve):
            dve.wait_ge(w_loaded, 16 * N_WLOADS)
            for h in range(HALVES):
                for k in range(TAPS):
                    last = dve.tensor_scalar(WSC[:, h * TAPS + k], WNAT[:, h], CW[:, h, k:k + 1], None, ALU.mult)
            last.then_inc(set_dve, 1)
            dve.memset(LESS[:, :], 0.0).then_inc(less_set, 1)
            dve.wait_ge(less_set, 1)
            dve.memset(LESS[BC:2 * BC, 0:1], -1.0)
            dve.memset(LESS[2 * BC:3 * BC, :], -1.0).then_inc(less_set, 1)
            dve.wait_ge(less_set, 2)
            dve.wait_ge(set_pe, 3)
            dve.tensor_tensor(TUC, DA[:, 0, 0:2], CB_[:, :], ALU.add).then_inc(set_dve, 1)
            dve.wait_ge(set_dve, 2)
            dve.tensor_scalar(TUC, TUC, NEG_LIMIT, None, ALU.max).then_inc(set_dve, 1)
            dve.wait_ge(set_act, 7)
            dve.tensor_tensor(TU, TUC, TSG, ALU.mult).then_inc(set_dve, 1)
            dve.wait_ge(set_dve, 4)
            dve.tensor_copy(UB, TU.unsqueeze(2).broadcast_to([P, HALVES, P])).then_inc(set_dve, 1)
            dve.wait_ge(set_act, 12)
            dve.tensor_tensor(TL, TL, TR, ALU.mult).then_inc(set_dve, 1)
            dve.wait_ge(set_act, 14)
            dve.scalar_tensor_tensor(out=TL, in0=TR, scalar=LOG_D, in1=TL, op0=ALU.add, op1=ALU.mult)\
                .then_inc(set_dve, 1)
            dve.wait_ge(set_dve, 7)
            dve.scalar_tensor_tensor(out=TL, in0=TS, scalar=LOG_H, in1=TL, op0=ALU.add, op1=ALU.mult)\
                .then_inc(set_dve, 1)
            dve.wait_ge(set_pe, 5)
            dve.wait_ge(set_dve, 8)
            dve.scalar_tensor_tensor(out=TDT, in0=DA[:, 0, 40:42], scalar=0.0, in1=TL, op0=ALU.max, op1=ALU.add)\
                .then_inc(set_dve, 1)
            dve.wait_ge(set_dve, 9)
            dve.tensor_tensor(TDU, TDT, TU, ALU.mult).then_inc(set_dve, 1)
            dve.wait_ge(set_dve, 10)
            for h in range(HALVES):
                last = dve.tensor_scalar(CAR[:, 0:NS * HALVES].rearrange("p (n h) -> p n h", h=HALVES)[:, :, h],
                                         DA[:, 0, 16:32], TDU[:, h:h + 1], None, ALU.mult)
            last.then_inc(set_dve, 1)
            dve.wait_ge(set_dve, 11)
            dve.tensor_copy(CAR[:, NS * HALVES:BATCH * NS * HALVES].rearrange("p (b n) -> p b n", b=BATCH - 1),
                            CAR[:, 0:NS * HALVES].unsqueeze(1).broadcast_to([P, BATCH - 1, NS * HALVES]))\
                .then_inc(car_saved, 4 * BATCH)

            def drive(unit, par, n, N):
                positive(dve, m_ready, N - HRING + 1)
                dve.wait_ge(b_ready, NDVE * unit + dve_index(n) + 1)
                dve.tensor_tensor(HB[:, n % HRING], DTU[:, par], over_halves(BB[:, 0:T]), ALU.mult)\
                    .then_inc(dbu_dve, 1)

            def step(J, par, s, main, front, back, prev, norm):
                f, k, g, N = J + 1, J - 1, J + 2, NS * J + s
                fp = kp = 1 - par
                if back and s == LAG:
                    dve.wait_ge(ysum_done, NS * (k + 1))
                    positive(dve, op_ready, k)
                    for h in range(HALVES):
                        last = dve.scalar_tensor_tensor(out=VV[:, h], in0=U[:, kp, h], scalar=DV[:, h:h + 1],
                                                        in1=Yp[:, h, 0:T], op0=ALU.mult, op1=ALU.add)
                    last.then_inc(v_ready, 1)
                if s % GRP == 1 and (main and s > 1 or prev and s == 1):
                    g = (s // GRP - 1) % GRP
                    unit = J if s > 1 else J - 1
                    dve.wait_ge(scan_done, 2 * (N - 1))
                    dve.tensor_copy(CAR[:, ds((unit + BATCH) * NS * HALVES + g * GRP * HALVES, GRP * HALVES)]
                                    .rearrange("p (n h) -> p n h", h=HALVES),
                                    HB[:, (g % 2) * GRP:(g % 2) * GRP + GRP, :, T - 1]).then_inc(car_saved, 1)
                if main:
                    if s + 1 < NS and s + 1 not in POOL_STATES:
                        drive(J, par, s + 1, N + 1)
                    elif s + 1 == NS and front:
                        dve.wait_ge(dtu_ready, J + 2)
                        drive(J + 1, 1 - par, 0, N + 1)
                    if s in POOL_STATES:
                        dve.wait_ge(dbu_pool, NPOOL * J + pool_index(s) + 1)
                    else:
                        dve.wait_ge(dbu_dve, NDVE * J + dve_index(s) + 1)
                    dve.wait_ge(car_saved, 4 * J + s // GRP + 1)
                    for h in range(HALVES):
                        dve.wait_ge(da_ready, 2 * N + h + 1)
                        dve.tensor_tensor_scan(HB[:, s % HRING, h], DA[:, h, 0:T], HB[:, s % HRING, h],
                                               CAR[:, ds(J * NS * HALVES + s * HALVES + h, 1)],
                                               ALU.mult, ALU.add).then_inc(scan_done, 1)
                if front and s in (2, 3):
                    h = s - 2
                    dve.wait_ge(conv_ready, 2 * f + h + 1)
                    dve.tensor_scalar(PP[:, h, 0:T], PP[:, h, 0:T], CB_[:, h:h + 1], NEG_LIMIT, ALU.add, ALU.max)\
                        .then_inc(clamped, 1)
                if front and s == 5:
                    dve.wait_ge(sg_ready, f + 1)
                    dve.tensor_tensor(U[:, fp], PPT, SG[:, :, :], ALU.mult).then_inc(u_ready, 1)
                if back and s == 7:
                    dve.wait_ge(op_ready, k + 1)
                    for r1 in range(2):
                        xr = by_row_parity(unit_x(k), r1)
                        last = dve.tensor_tensor(xr, xr, seq_rows(PP[:, 0, 0:T], r1), ALU.add)
                    last.then_inc(x2_ready, 1)
                if front and s == 7:
                    dve.wait_ge(hi_ready, f + 1)
                    dve.scalar_tensor_tensor(out=PP[0:DTROW, 1, 0:T], in0=PART[:, :], scalar=LESS[:, 0:1],
                                             in1=PP[0:DTROW, 1, 0:T], op0=ALU.mult, op1=ALU.add)\
                        .then_inc(res_ready, 1)
                if back and s == 9:
                    dve.wait_ge(mean2_ready, k + 1)
                    positive(dve, out_ready, k)
                    dve.tensor_tensor(XC2[:, :, :], unit_x(k), over_q(STAT), ALU.subtract).then_inc(xc2_ready, 1)
                if front and s == 8:
                    dve.wait_ge(mid_ready, f + 1)
                    dve.scalar_tensor_tensor(out=PT[:, fp], in0=PART[:, :], scalar=LESS[:, 1:2],
                                             in1=PP[0:DTROW, 1, 0:T], op0=ALU.mult, op1=ALU.add)\
                        .then_inc(parts_ready, 1)
                if norm and s == 3:
                    dve.wait_ge(mean_ready, g + 1)
                    positive(dve, xn_ready, g)
                    dve.tensor_tensor(XC[:, :, :], unit_x(g), over_q(STAT), ALU.subtract).then_inc(xc_ready, 1)
                if front and s == 12:
                    dve.wait_ge(r2_ready, 2 * f + 1)
                    dve.scalar_tensor_tensor(out=SE[:, :, :], in0=SR[:, :, :], scalar=LOG_D, in1=SE[:, :, :],
                                             op0=ALU.add, op1=ALU.mult).then_inc(m1_done, 1)
                    dve.wait_ge(r2_ready, 2 * f + 2)
                    dve.wait_ge(m1_done, 2 * f + 1)
                    dve.scalar_tensor_tensor(out=SE[:, :, :], in0=SS[:, :, :], scalar=LOG_H, in1=SE[:, :, :],
                                             op0=ALU.add, op1=ALU.mult).then_inc(m1_done, 1)
                    dve.wait_ge(m1_done, 2 * f + 2)
                    dve.scalar_tensor_tensor(out=DT[:, fp], in0=PPT, scalar=0.0, in1=SE[:, :, :],
                                             op0=ALU.max, op1=ALU.add).then_inc(dt_ready, 1)
                if main and s == 13:
                    dve.wait_ge(z_ready, J + 1)
                    dve.tensor_scalar(PPT, PPT, NEG_LIMIT, None, ALU.max).then_inc(z_clamped, 1)
                if main and s == 15:
                    dve.wait_ge(sgz_ready, J + 1)
                    positive(dve, vg_ready, J)
                    dve.tensor_tensor(GZ[:, :, :], PPT, SGZ[:, :, :], ALU.mult).then_inc(gz_ready, 1)

            def first_main():
                dve.wait_ge(dtu_ready, 1)
                drive(0, 0, 0, 0)

            run_units(dve, step, first_main)

            X0v = X[:, 0:BATCH * T].rearrange("p (b q t) -> p q b t", b=BATCH, q=Q)[:, :, :, 0]
            dve.wait_ge(f_pe, 1)
            dve.tensor_tensor(x0, X0v, PP[:, 0, 0:4].unsqueeze(1).broadcast_to([P, Q, BATCH]), ALU.subtract)\
                .then_inc(f_dve, 1)
            dve.wait_ge(f_act, 3)
            dve.tensor_tensor(x0, x0, r0.unsqueeze(1).broadcast_to([P, Q, BATCH]), ALU.mult).then_inc(f_dve, 1)
            dve.wait_ge(f_pe, 3)
            dve.tensor_copy(SCO, PP[0:BATCH, 1, 0:MEM]).then_inc(f_dve, 1)
            dve.wait_ge(f_dve, 3)
            dve.max(TOP, SCO).then_inc(f_dve, 1)
            dve.wait_ge(f_dve, 4)
            dve.tensor_scalar(NMX, TOP[:, 0:1], -1.0, None, ALU.mult).then_inc(f_dve, 1)
            dve.max_index(IDX[:, :], TOP, SCO).then_inc(idx_ready, 1)
            dve.wait_ge(f_act, 4)
            dve.reciprocal(WRC, WSUM).then_inc(f_dve, 1)
            dve.wait_ge(f_dve, 6)
            dve.tensor_scalar(WNM, WEX, WRC, None, ALU.mult).then_inc(f_dve, 1)
            dve.wait_ge(f_dve, 7)
            dve.tensor_tensor(WDG, IDENT[0:BATCH, 0:BATCH].unsqueeze(2).broadcast_to([BATCH, BATCH, TOPK]),
                              WNM.unsqueeze(1).broadcast_to([BATCH, BATCH, TOPK]), ALU.mult).then_inc(f_dve, 1)
            dve.wait_ge(f_pe, 4)
            dve.tensor_copy(WBC, PP[:, 0, 16:48]).then_inc(f_dve, 1)
            dve.wait_ge(f_dve, 9)
            dve.tensor_tensor(WI, IDENT[:, :].unsqueeze(1).broadcast_to([P, BATCH * TOPK, P]),
                              WBC.unsqueeze(2).broadcast_to([P, BATCH * TOPK, P]), ALU.mult).then_inc(f_dve, 1)
            for b in range(BATCH):
                ps = (Yp[:, b % 2] if b < 2 else DA[:, b % 2]).rearrange("p (q t) -> p q t", q=Q)
                dve.wait_ge(g_used, b + 1)
                o0 = unit_seq(b).rearrange("p (q t) -> p q t", q=Q)
                o1 = unit_seq(BATCH + b).rearrange("p (q t) -> p q t", q=Q)
                dve.tensor_tensor(o0[:, :, 1:TOK], unit_x(b)[:, :, 1:TOK], ps[:, :, 0:TOK - 1], ALU.add)
                rest = MT - (TOK - 1)
                dve.tensor_tensor(o1[:, :, 0:rest], unit_x(BATCH + b)[:, :, 0:rest], ps[:, :, TOK - 1:MT], ALU.add)\
                    .then_inc(comb_done, 1)


_NAMES = ["x", "L0_conv_global_token", "L0_conv_in_proj_w", "L0_conv_conv_w", "L0_conv_conv_b",
          "L0_conv_x_proj_w", "L0_conv_dt_proj_w", "L0_conv_dt_proj_b", "L0_conv_A_log", "L0_conv_D",
          "L0_conv_out_proj_w", "L0_ffn_memory_tokens", "L0_ffn_memory_router"]


def kernel(**inputs):
    import numpy as np
    import concourse.bacc as bacc
    from concourse.bass_utils import run_bass_kernel_spmd as run

    nc = bacc.Bacc("TRN2", target_bir_lowering=False, num_devices=1)
    arrays, args = {}, []
    for name in _NAMES:
        a = np.ascontiguousarray(inputs[name])
        arrays[f"in_{name}"] = a
        args.append(nc.dram_tensor(f"in_{name}", a.shape, mybir.dt.from_np(a.dtype), kind="ExternalInput").ap())
    shape = inputs["x"].shape
    result = nc.dram_tensor("out_0", shape, F32, kind="ExternalOutput").ap()
    build(nc, *args, result)
    r = run(nc, [arrays], core_ids=[0])
    return r.results[0]["out_0"]
```

```python
from contextlib import ExitStack

import concourse.bass as bass
from concourse import mybir
from concourse.bass import ds

F32 = mybir.dt.float32
BF16 = mybir.dt.bfloat16
U32 = mybir.dt.uint32
ACT = mybir.ActivationFunctionType
ALU = mybir.AluOpType

P = 128
BATCH, DIM, HH, WW = 4, 512, 24, 24
Q = DIM // P
HALVES = 2
NS = 16
RANK = 8
TAPS = 4
HIST = TAPS - 1
ROWS = 4
CHUNKS = HH // ROWS
TOK = ROWS * WW
T = TOK * Q
UNITS = CHUNKS * BATCH
SLOT = HIST + T
TOPK = 8
MEM, MT = 256, 128
BC = 2 * NS
PARTS = 3
DTROW = PARTS * BC
XROWS = DTROW + RANK
XP_M = XROWS
NEG_LIMIT = -44.0
EPS_C, EPS_T = 1e-6, 1e-5
LOG_C, LOG_D, LOG_G, LOG_H = 0.34222454, 1.83313539, 0.33814541, 1.75319741 ** 2
POOL_STATES = (3, 5, 7, 9)
NPOOL = len(POOL_STATES)
NDVE = NS - NPOOL
HRING, MRING, CRING = 8, 4, 4
LAG = 3
GRP = 4

STAGES_PER_UNIT = NS + NPOOL


def dve_index(n):
    return sum(1 for m in range(n) if m not in POOL_STATES)


def pool_index(n):
    return POOL_STATES.index(n)


def staged(s):
    return [("B", s + 3)] * (s + 3 in POOL_STATES) + [("C", s + 2)]


def stage_index(kind, n):
    order = [("C", 0), ("C", 1)] + [use for s in range(NS - 2) for use in staged(s)]
    return order.index((kind, n))


def build(nc, x, tok, w_in, conv_w, conv_b, xp_w, dt_w, dt_b, a_log, dvec, op_w, mem, router, out):
    ctx = ExitStack()
    with ctx:
        def sb(name, shape, dt=F32):
            return ctx.enter_context(nc.sbuf_tensor(name, shape, dt))

        def sem(name):
            return ctx.enter_context(nc.semaphore(name))

        X = sb("X", [P, UNITS * T])
        XN = sb("XN", [P, (UNITS + BATCH) * SLOT])
        CAR = sb("CAR", [P, (UNITS + BATCH) * NS * HALVES])
        SCAN = sb("SCAN", [P, (HRING + MRING) * HALVES * T])
        HB = SCAN[:, 0:HRING * HALVES * T].rearrange("p (r h t) -> p r h t", r=HRING, h=HALVES)
        M = SCAN[:, HRING * HALVES * T:].rearrange("p (r h t) -> p r h t", r=MRING, h=HALVES)
        UDT = sb("UDT", [P, 6 * HALVES * T])
        UDTv = UDT[:, :].rearrange("p (k r h t) -> p k r h t", k=3, r=2, h=HALVES)
        U, DT, DTU = (UDTv[:, k] for k in range(3))
        CS = sb("CS", [P, CRING, T])
        BS = sb("BS", [P, 2, T])
        XC = sb("XC", [P, Q, TOK]); SQ = sb("SQ", [P, Q, TOK])
        LNV = sb("LNV", [P, TOK]); RSTD = sb("RSTD", [P, TOK])
        XC2 = sb("XC2", [P, Q, TOK]); SQ2 = sb("SQ2", [P, Q, TOK])
        LNV2 = sb("LNV2", [P, TOK]); RSTD2 = sb("RSTD2", [P, TOK])
        SG = sb("SG", [P, HALVES, T])
        SGZ = sb("SGZ", [P, HALVES, T])
        SE = sb("SE", [P, HALVES, T])
        SR = sb("SR", [P, HALVES, T])
        SS = sb("SS", [P, HALVES, T])
        GZ = sb("GZ", [P, HALVES, T])
        VV = sb("VV", [P, HALVES, T])
        PT = sb("PT", [DTROW, 2, T], BF16)
        PART = sb("PART", [DTROW, T], BF16)
        LESS = sb("LESS", [DTROW, PARTS - 1])
        XDT = sb("XDT", [P, T])
        WT = sb("WT", [P, HALVES, TAPS, P])
        WZT = sb("WZT", [P, HALVES, P])
        XPT = sb("XPT", [P, HALVES, XP_M])
        DTW = sb("DTW", [P, HALVES, P])
        OPT = sb("OPT", [P, HALVES, P])
        DD = sb("DD", [P, HALVES, P])
        IDENT = sb("IDENT", [P, P]); MEANW = sb("MEANW", [P, P])
        SEL = sb("SEL", [DTROW, BC, P], BF16)
        A = sb("A", [P, HALVES, NS]); AE = sb("AE", [P, HALVES, NS])
        CB_ = sb("conv_bias", [P, HALVES]); DV = sb("DV", [P, HALVES])
        CW = sb("CW", [P, HALVES, TAPS])
        EPSC = sb("EPSC", [P, 1]); EPST = sb("EPST", [P, 1])
        LOGB = sb("LOGB", [P, 2])
        RW = sb("RW", [P, Q, MEM])
        WNAT = SCAN[:, 0:512].rearrange("p (k c) -> p k c", k=4)
        WSC = SCAN[:, 512:1536].rearrange("p (k c) -> p k c", k=8)
        OPNAT = SCAN[:, 1536:1792]
        XPNAT = SCAN[0:RANK + BC, 1792:2048]
        DTNAT = SCAN[:, 2048:2048 + 2 * (XROWS + 1)].rearrange("p (k c) -> p k c", k=2)
        TKC = SCAN[:, 2304:2305]
        TU = SCAN[:, 2306:2308]; TSG = SCAN[:, 2308:2310]; TUC = SCAN[:, 2310:2312]
        TL = SCAN[:, 2312:2314]; TR = SCAN[:, 2576:2578]; TS = SCAN[:, 2578:2580]; TDT = SCAN[:, 2314:2316]; TDU = SCAN[:, 2316:2318]
        UB = SCAN[:, 2320:2576].rearrange("p (k c) -> p k c", k=2)
        GR = 16
        G = SCAN[:, 0:GR * DIM].rearrange("p (r d) -> p r d", r=GR)
        WI = UDT[:, 0:BATCH * TOPK * P].rearrange("p (k t) -> p k t", t=P)
        x0 = SCAN[:, GR * DIM:GR * DIM + 16].rearrange("p (q b) -> p q b", q=Q)
        x0s = SCAN[:, GR * DIM + 16:GR * DIM + 32].rearrange("p (q b) -> p q b", q=Q)
        r0 = SCAN[:, GR * DIM + 32:GR * DIM + 36]
        SCO = SCAN[0:BATCH, GR * DIM + 64:GR * DIM + 64 + MEM]
        TOP = SCAN[0:BATCH, GR * DIM + 320:GR * DIM + 328]
        NMX = SCAN[0:BATCH, GR * DIM + 328:GR * DIM + 329]
        WEX = SCAN[0:BATCH, GR * DIM + 336:GR * DIM + 344]
        WSUM = SCAN[0:BATCH, GR * DIM + 344:GR * DIM + 345]
        WRC = SCAN[0:BATCH, GR * DIM + 345:GR * DIM + 346]
        WNM = SCAN[0:BATCH, GR * DIM + 352:GR * DIM + 360]
        WDG = SCAN[0:BATCH, GR * DIM + 360:GR * DIM + 392].rearrange("p (b k) -> p b k", b=BATCH)
        WBC = SCAN[:, GR * DIM + 400:GR * DIM + 432]
        IDX = sb("IDX", [BATCH, TOPK], U32)
        ONE4 = sb("ONE4", [BATCH, P])

        Yp = ctx.enter_context(nc.psum_tensor("Yp", [P, HALVES, 512], F32))
        DA = ctx.enter_context(nc.psum_tensor("DA", [P, HALVES, 512], F32))
        BB = ctx.enter_context(nc.psum_tensor("BB", [P, 512], F32))
        ST = ctx.enter_context(nc.psum_tensor("ST", [P, 512], F32))
        PP = ctx.enter_context(nc.psum_tensor("PP", [P, HALVES, 512], F32))
        STAT = PP[:, 1, 0:TOK]; STAT2 = PP[:, 0, 0:TOK]
        PPT = PP[:, :, 0:T]

        w_loaded = sem("w_loaded"); x_loaded = sem("x_loaded")
        x_first = [sem(f"x_first{b}") for b in range(BATCH)]
        ffn_loaded = sem("ffn_loaded")
        const_ready = sem("const_ready")
        zeroed = sem("zeroed")
        less_set = sem("less_set")
        set_pe = sem("set_pe"); set_act = sem("set_act"); set_dve = sem("set_dve")
        mean_ready = sem("mean_ready"); xc_ready = sem("xc_ready"); sq_ready = sem("sq_ready")
        var_ready = sem("var_ready"); ln_done = sem("ln_done"); rstd_ready = sem("rstd_ready")
        xn_part = sem("xn_part"); xn_ready = sem("xn_ready")
        conv_ready = sem("conv_ready"); clamped = sem("clamped"); sg_chain = sem("sg_chain")
        sg_ready = sem("sg_ready"); u_ready = sem("u_ready"); xp_ready = sem("xp_ready")
        hi_ready = sem("hi_ready"); res_ready = sem("res_ready"); mid_ready = sem("mid_ready")
        parts_ready = sem("parts_ready"); dtp_ready = sem("dtp_ready"); sp_chain = sem("sp_chain")
        relu_done = sem("relu_done"); sq_e_ready = sem("sq_e_ready"); cr_ready = sem("cr_ready"); r2_ready = sem("r2_ready"); m1_done = sem("m1_done"); dt_ready = sem("dt_ready"); dtu_ready = sem("dtu_ready")
        b_ready = sem("b_ready"); dbu_dve = sem("dbu_dve"); dbu_pool = sem("dbu_pool")
        st_ready = sem("st_ready"); st_copied = sem("st_copied")
        da_ready = sem("da_ready"); scan_done = sem("scan_done"); car_saved = sem("car_saved")
        m_ready = sem("m_ready"); ysum_done = sem("ysum_done")
        z_ready = sem("z_ready"); z_clamped = sem("z_clamped"); sgz_chain = sem("sgz_chain")
        sgz_ready = sem("sgz_ready"); gz_ready = sem("gz_ready"); v_ready = sem("v_ready")
        op_ready = sem("op_ready"); x2_ready = sem("x2_ready")
        mean2_ready = sem("mean2_ready"); xc2_ready = sem("xc2_ready"); sq2_ready = sem("sq2_ready")
        var2_ready = sem("var2_ready"); ln2_done = sem("ln2_done"); rstd2_ready = sem("rstd2_ready")
        xh2_done = sem("xh2_done"); out_ready = sem("out_ready"); stored = sem("stored")
        f_pe = sem("f_pe"); f_act = sem("f_act"); f_dve = sem("f_dve")
        idx_ready = sem("idx_ready"); g_loaded = [sem(f"g_loaded{b}") for b in range(BATCH)]
        g_used = sem("g_used"); comb_done = sem("comb_done")

        N_WLOADS = 11
        block = ctx.enter_context(nc.Block())

        def unit_x(j):
            return X[:, ds(j * T, T)].rearrange("p (q t) -> p q t", q=Q)

        def unit_seq(j):
            return XN[:, ds(j * SLOT + HIST, T)]

        def by_row_parity(ap_qt, r1):
            return ap_qt[:, 2 * r1:2 * r1 + 2, :].rearrange("p r (h w) -> p h w r", w=WW)

        def seq_rows(ap_t, r1):
            return ap_t.rearrange("p (h r w s) -> p h r w s", h=ROWS, r=2, w=WW)[:, :, r1]

        def over_q(ap):
            return ap.unsqueeze(1).broadcast_to([P, Q, TOK])

        def over_halves(ap):
            return ap.unsqueeze(1).broadcast_to([P, HALVES, T])

        def positive(eng, s, v):
            if isinstance(v, int) and v <= 0:
                return
            assert isinstance(v, int) or v.min_val > 0
            eng.wait_ge(s, v)

        def run_units(eng, step, first_main=None):
            def unit(J, par, main=True, front=True, back=True, conv=True, norm=True):
                prev = back
                for s in range(NS):
                    step(J, par, s, main, front, back, prev, conv, norm)
            unit(-3, 1, main=False, front=False, back=False, conv=False)
            unit(-2, 0, main=False, front=False, back=False)
            unit(-1, 1, main=False, back=False)
            if first_main:
                first_main()
            unit(0, 0, back=False)
            unit(1, 1)
            with eng.Fori(1, (UNITS - 4) // 2) as i:
                unit(2 * i, 0)
                unit(2 * i + 1, 1)
            unit(UNITS - 4, 0)
            unit(UNITS - 3, 1, norm=False)
            unit(UNITS - 2, 0, conv=False, norm=False)
            unit(UNITS - 1, 1, front=False, conv=False, norm=False)
            unit(UNITS, 0, main=False, front=False, conv=False, norm=False)

        @block.sync
        def _(sp):
            xv = x.rearrange("b (p q) (c s) w -> c p b q (s w)", q=Q, s=ROWS)
            ov = out.rearrange("b (p q) (c s) w -> c b p q (s w)", q=Q, s=ROWS)
            Xc = X[:, :].rearrange("p (c b q t) -> p c b q t", c=CHUNKS, b=BATCH, q=Q)
            sp.dma_start(WNAT, w_in.rearrange("(k e) c -> e k c", e=P)).then_inc(w_loaded, 16)
            sp.dma_start(Xc[:, 0, 0], xv[0, :, 0]).then_inc(x_first[0], 16)
            sp.dma_start(CW[:, :, :], conv_w.rearrange("(k e) t -> e k t", e=P)).then_inc(w_loaded, 16)
            sp.dma_start(OPNAT, op_w).then_inc(w_loaded, 16)
            sp.dma_start(XPNAT, xp_w).then_inc(w_loaded, 16)
            sp.dma_start(CB_[:, :], conv_b.rearrange("(k e) -> e k", e=P), allow_slow_non_contiguous=True).then_inc(w_loaded, 16)
            sp.dma_start(DV[:, :], dvec.rearrange("(k e) -> e k", e=P), allow_slow_non_contiguous=True).then_inc(w_loaded, 16)
            sp.dma_start(AE[:, :, :], a_log.rearrange("(k e) n -> e k n", e=P)).then_inc(w_loaded, 16)
            sp.dma_start(TKC, tok.rearrange("a b c -> c (a b)"), allow_slow_non_contiguous=True).then_inc(w_loaded, 16)
            sp.wait_ge(zeroed, 1)
            sp.dma_start(DTNAT[:, :, DTROW:XROWS],
                         dt_w.rearrange("(k e) r -> e k r", e=P)).then_inc(w_loaded, 16)
            sp.dma_start(DTNAT[:, :, XROWS:XROWS + 1],
                         dt_b.rearrange("(k e r) -> e k r", e=P, r=1), allow_slow_non_contiguous=True).then_inc(w_loaded, 16)
            sp.dma_start(RW[:, :, :], router.rearrange("(p q) m -> p q m", q=Q)).then_inc(w_loaded, 16)
            for b in range(1, BATCH):
                sp.dma_start(Xc[:, 0, b], xv[0, :, b]).then_inc(x_first[b], 16)
            for c in range(1, CHUNKS):
                for b in range(BATCH):
                    sp.dma_start(Xc[:, c, b], xv[c, :, b]).then_inc(x_loaded, 16)

            def store(c, b, j):
                sp.wait_ge(out_ready, j + 1)
                sp.dma_start(ov[ds(c, 1), ds(b, 1)].rearrange("c b p q t -> (c b p) q t"),
                             unit_seq(j).rearrange("p (q t) -> p q t", q=Q)).then_inc(stored, 16)
            with sp.Fori(2, CHUNKS) as c:
                with sp.Fori(0, BATCH) as b:
                    store(c, b, c * BATCH + b)

            sp.wait_ge(idx_ready, 1)
            sp.wait_ge(ysum_done, NS * UNITS)
            for b in range(BATCH):
                if b >= 2:
                    sp.wait_ge(g_used, b - 1)
                for k in range(TOPK):
                    m = sp.value_load(IDX[b:b + 1, k:k + 1], min_val=0, max_val=MEM - 1)
                    sp.dma_start(G[:, (b % 2) * TOPK + k, :],
                                 mem[ds(m, 1)].rearrange("a t d -> (a t) d")).then_inc(g_loaded[b], 16)
            sp.wait_ge(comb_done, BATCH)
            for c in range(2):
                for b in range(BATCH):
                    sp.dma_start(ov[c, b], unit_seq(c * BATCH + b).rearrange("p (q t) -> p q t", q=Q))\
                        .then_inc(stored, 16)
            sp.wait_ge(stored, 16 * UNITS)

        @block.gpsimd
        def _(pool):
            pool.memset(DTNAT, 0.0).then_inc(zeroed, 1)
            pool.memset(IDENT[:, :], 0.0).then_inc(zeroed, 1)
            pool.memset(SEL[:, :, :], 0.0).then_inc(zeroed, 1)
            pool.memset(MEANW[:, :], 1.0 / DIM).then_inc(const_ready, 1)
            pool.memset(XDT[:, :], 1.0).then_inc(const_ready, 1)
            pool.memset(EPSC[:, :], EPS_C).then_inc(const_ready, 1)
            pool.memset(EPST[:, :], EPS_T).then_inc(const_ready, 1)
            pool.memset(LOGB[:, 0:1], 2.0 / LOG_C).then_inc(const_ready, 1)
            pool.memset(LOGB[:, 1:2], -LOG_G).then_inc(const_ready, 1)
            pool.memset(ONE4[:, :], 1.0).then_inc(const_ready, 1)
            for b in range(BATCH):
                pool.memset(XN[:, b * SLOT:b * SLOT + HIST - 1], 0.0).then_inc(const_ready, 1)
            pool.wait_ge(zeroed, 3)
            pool.affine_select(out=IDENT[:, :], in_=IDENT[:, :], compare_op=ALU.not_equal, fill=1.0,
                               base=0, pattern=[[-1, P]], channel_multiplier=1).then_inc(const_ready, 1)
            for part in range(PARTS):
                if part:
                    pool.wait_ge(zeroed, 3 + part)
                pool.affine_select(out=SEL[:, :, :], in_=SEL[:, :, :], compare_op=ALU.not_equal, fill=1.0,
                                   base=-part * BC, pattern=[[-1, BC], [0, P]],
                                   channel_multiplier=1).then_inc(zeroed if part < PARTS - 1 else const_ready, 1)
            pool.wait_ge(w_loaded, 16 * N_WLOADS)
            for b in range(BATCH):
                pool.tensor_copy(XN[:, b * SLOT + HIST - 1:b * SLOT + HIST], TKC).then_inc(const_ready, 1)

            def step(J, par, s, main, front, back, prev, conv, norm):
                f, k, g, N = J + 1, J - 1, J + 3, NS * J + s
                fp = kp = 1 - par
                if main and (s > 0 or prev) or (s == 0 and prev):
                    n1 = (s - 1) % NS
                    unit1 = J if s else J - 1
                    pool.wait_ge(scan_done, 2 * N)
                    pool.wait_ge(st_copied, STAGES_PER_UNIT * unit1 + stage_index("C", n1) + 1)
                    positive(pool, ysum_done, N - MRING)
                    pool.tensor_tensor(M[:, n1 % MRING], HB[:, n1 % HRING],
                                       over_halves(CS[:, n1 % CRING]), ALU.mult).then_inc(m_ready, 1)
                if main and s + 2 in POOL_STATES:
                    n2 = s + 2
                    pool.wait_ge(st_copied, STAGES_PER_UNIT * J + stage_index("B", n2) + 1)
                    pool.wait_ge(dtu_ready, J + 1)
                    pool.wait_ge(car_saved, 4 * BATCH + 4 * J + (n2 - HRING) // GRP + 1)
                    pool.tensor_tensor(HB[:, n2 % HRING], DTU[:, par], over_halves(BS[:, pool_index(n2) % 2]),
                                       ALU.mult).then_inc(dbu_pool, 1)
                if front and s == 11:
                    pool.wait_ge(sq_e_ready, f + 1)
                    pool.tensor_tensor(SE[:, :, :], SE[:, :, :], SR[:, :, :], ALU.mult).then_inc(cr_ready, 1)
                if back and s == 13:
                    pool.wait_ge(rstd2_ready, k + 1)
                    pool.tensor_tensor(XC2[:, :, :], XC2[:, :, :], over_q(RSTD2[:, :]), ALU.mult)\
                        .then_inc(xh2_done, 1)
                if back and s == 14:
                    pool.wait_ge(xh2_done, k + 1)
                    pool.tensor_tensor(unit_seq(k).rearrange("p (q t) -> p q t", q=Q), XC2[:, :, :], unit_x(k),
                                       ALU.add).then_inc(out_ready, 1)
                if front and s == 13:
                    pool.wait_ge(dt_ready, f + 1)
                    pool.tensor_tensor(DTU[:, fp], DT[:, fp], U[:, fp], ALU.mult).then_inc(dtu_ready, 1)
                if norm and s == 15:
                    pool.wait_ge(rstd_ready, g + 1)
                    for r1 in range(2):
                        pool.tensor_tensor(seq_rows(unit_seq(g), r1), by_row_parity(XC[:, :, :], r1),
                                           by_row_parity(over_q(RSTD[:, :]), r1), ALU.mult).then_inc(xn_part, 1)
                    pool.wait_ge(xn_part, 2 * (g + 1))
                    pool.tensor_copy(XN[:, ds((g + BATCH) * SLOT, HIST)],
                                     XN[:, ds(g * SLOT + T, HIST)]).then_inc(xn_ready, 1)

            run_units(pool, step)

        @block.scalar
        def _(act):
            act.preload_act_table_set("natural_log_exp_and_others")
            act.wait_ge(w_loaded, 16 * N_WLOADS)
            act.wait_ge(const_ready, 7)
            act.activation(A[:, :, :], AE[:, :, :], ACT.Exp).then_inc(set_act, 1)
            act.wait_ge(set_act, 1)
            act.activation(A[:, :, :], A[:, :, :], ACT.Copy, scale=-1.0).then_inc(set_act, 1)
            act.wait_ge(set_pe, 1)
            act.activation(WT[:, :, :, :].rearrange("p h k c -> p h (k c)"), Yp[:, :, :], ACT.Copy)\
                .then_inc(set_act, 1)
            act.wait_ge(set_pe, 2)
            act.activation(WZT[:, :, :].rearrange("p h c -> p (h c)"), PP[:, 0, 0:256], ACT.Copy)
            act.activation(OPT[:, :, :].rearrange("p h c -> p (h c)"), PP[:, 0, 256:512], ACT.Copy)
            for h in range(HALVES):
                xp = PP[:, 1, h * 40:h * 40 + 40]
                for part in range(PARTS):
                    act.activation(XPT[:, h, part * BC:(part + 1) * BC], xp[:, RANK:RANK + BC], ACT.Copy)
                act.activation(XPT[:, h, DTROW:XROWS], xp[:, 0:RANK], ACT.Copy)
                last = act.activation(DTW[DTROW:XROWS + 1, h], PP[DTROW:XROWS + 1, 1, 128 + h * P:256 + h * P],
                                      ACT.Copy)
            last.then_inc(set_act, 1)
            act.wait_ge(set_dve, 3)
            act.activation(TSG, TUC, ACT.Exp, scale=-1.0).then_inc(set_act, 1)
            act.wait_ge(set_act, 5)
            act.activation(TSG, TSG, ACT.Ln, bias=1.0).then_inc(set_act, 1)
            act.wait_ge(set_act, 6)
            act.activation(TSG, TSG, ACT.Exp, scale=-1.0).then_inc(set_act, 1)
            act.wait_ge(set_pe, 4)
            act.activation(XDT[DTROW:XROWS, 0:1], DA[DTROW:XROWS, 0, 8:9], ACT.Copy).then_inc(set_act, 1)
            act.wait_ge(set_pe, 5)
            act.activation(TL, DA[:, 0, 40:42], ACT.Abs).then_inc(set_act, 1)
            act.wait_ge(set_act, 9)
            act.activation(TL, TL, ACT.Exp, scale=-1.0).then_inc(set_act, 1)
            act.wait_ge(set_act, 10)
            act.activation(TR, TL, ACT.Ln, bias=LOGB[:, 0:1], scale=1.0 / LOG_C).then_inc(set_act, 1)
            act.wait_ge(set_act, 11)
            act.activation(TR, TR, ACT.Exp, scale=-1.0).then_inc(set_act, 1)
            act.wait_ge(set_dve, 6)
            act.activation(TR, TL, ACT.Square, scale=1.0 / LOG_C).then_inc(set_act, 1)
            act.wait_ge(set_act, 13)
            act.activation(TS, TR, ACT.Square, bias=LOGB[:, 1:2]).then_inc(set_act, 1)

            def decay(J, par, n, N, h):
                positive(act, scan_done, 2 * N - 1 + h)
                act.activation(DA[:, h, 0:T], DT[:, par, h], ACT.Exp, scale=A[:, h, n:n + 1])\
                    .then_inc(da_ready, 1)

            def step(J, par, s, main, front, back, prev, conv, norm):
                f, k, g, N = J + 1, J - 1, J + 3, NS * J + s
                fp = kp = 1 - par
                if main:
                    if s < NS - 1:
                        unit, upar, n1 = J, par, s + 1
                    else:
                        unit, upar, n1 = J + 1, 1 - par, 0
                    if s < NS - 1 or front:
                        if n1 == 0:
                            act.wait_ge(dt_ready, unit + 1)
                        decay(unit, upar, n1, N + 1, 0)
                        act.wait_ge(st_ready, STAGES_PER_UNIT * unit + stage_index("C", n1) + 1)
                        positive(act, m_ready, N + 2 - CRING)
                        act.activation(CS[:, n1 % CRING], ST[:, 0:T], ACT.Copy).then_inc(st_copied, 1)
                        decay(unit, upar, n1, N + 1, 1)
                    for n in [n for kind, n in staged(s) if kind == "B"]:
                        act.wait_ge(st_ready, STAGES_PER_UNIT * J + stage_index("B", n) + 1)
                        positive(act, dbu_pool, NPOOL * J + pool_index(n) - 1)
                        act.activation(BS[:, pool_index(n) % 2], ST[:, 0:T], ACT.Copy).then_inc(st_copied, 1)
                if front and s == 1:
                    act.wait_ge(clamped, 2 * f + 2)
                    positive(act, u_ready, f)
                    act.activation(SG[:, :, :], U[:, fp], ACT.Exp, scale=-1.0).then_inc(sg_chain, 1)
                if front and s == 2:
                    act.wait_ge(sg_chain, 2 * f + 1)
                    act.activation(SG[:, :, :], SG[:, :, :], ACT.Ln, bias=1.0).then_inc(sg_chain, 1)
                    act.wait_ge(sg_chain, 2 * f + 2)
                    act.activation(SG[:, :, :], SG[:, :, :], ACT.Exp, scale=-1.0).then_inc(sg_ready, 1)
                if front and s == 4:
                    act.wait_ge(xp_ready, f + 1)
                    positive(act, parts_ready, f)
                    act.activation(PART[:, :], PP[0:DTROW, 1, 0:T], ACT.Copy)
                    act.activation(XDT[DTROW:XROWS, :], PP[DTROW:XROWS, 1, 0:T], ACT.Copy).then_inc(hi_ready, 1)
                if front and s == 6:
                    act.wait_ge(res_ready, f + 1)
                    act.activation(PART[:, :], PP[0:DTROW, 1, 0:T], ACT.Copy).then_inc(mid_ready, 1)
                if front and s == 8:
                    act.wait_ge(dtp_ready, f + 1)
                    positive(act, dt_ready, f)
                    act.activation(SE[:, :, :], PPT, ACT.Abs).then_inc(sp_chain, 1)
                    act.activation(DT[:, fp], PPT, ACT.Relu).then_inc(relu_done, 1)
                if front and s == 9:
                    act.wait_ge(sp_chain, 3 * f + 1)
                    act.activation(SE[:, :, :], SE[:, :, :], ACT.Exp, scale=-1.0).then_inc(sp_chain, 1)
                    act.wait_ge(sp_chain, 3 * f + 2)
                    act.activation(SR[:, :, :], SE[:, :, :], ACT.Ln, bias=LOGB[:, 0:1], scale=1.0 / LOG_C)\
                        .then_inc(sp_chain, 1)
                if front and s == 10:
                    act.wait_ge(sp_chain, 3 * f + 3)
                    act.activation(SR[:, :, :], SR[:, :, :], ACT.Exp, scale=-1.0).then_inc(sq_e_ready, 1)
                if back and s == 11:
                    act.wait_ge(xc2_ready, k + 1)
                    act.activation(SQ2[:, :, :], XC2[:, :, :], ACT.Square).then_inc(sq2_ready, 1)
                if front and s == 12:
                    act.wait_ge(cr_ready, f + 1)
                    act.activation(SR[:, :, :], SE[:, :, :], ACT.Square, scale=1.0 / LOG_C).then_inc(r2_ready, 1)
                    act.wait_ge(r2_ready, 2 * f + 1)
                    act.activation(SS[:, :, :], SR[:, :, :], ACT.Square, bias=LOGB[:, 1:2]).then_inc(r2_ready, 1)
                if back and s == 12:
                    act.wait_ge(var2_ready, k + 1)
                    act.activation(LNV2[:, :], STAT2, ACT.Ln, bias=EPST[:, 0:1]).then_inc(ln2_done, 1)
                    act.wait_ge(ln2_done, k + 1)
                    positive(act, out_ready, k)
                    act.activation(RSTD2[:, :], LNV2[:, :], ACT.Exp, scale=-0.5).then_inc(rstd2_ready, 1)
                if norm and s == 11:
                    act.wait_ge(xc_ready, g + 1)
                    positive(act, var_ready, g)
                    act.activation(SQ[:, :, :], XC[:, :, :], ACT.Square).then_inc(sq_ready, 1)
                if main and s == 13:
                    act.wait_ge(z_clamped, J + 1)
                    positive(act, gz_ready, J)
                    act.activation(SGZ[:, :, :], GZ[:, :, :], ACT.Exp, scale=-1.0).then_inc(sgz_chain, 1)
                if norm and s == 12:
                    act.wait_ge(var_ready, g + 1)
                    act.activation(LNV[:, :], STAT, ACT.Ln, bias=EPSC[:, 0:1]).then_inc(ln_done, 1)
                    act.wait_ge(ln_done, g + 1)
                    positive(act, xn_ready, g)
                    act.activation(RSTD[:, :], LNV[:, :], ACT.Exp, scale=-0.5).then_inc(rstd_ready, 1)
                if main and s == 14:
                    act.wait_ge(sgz_chain, 2 * J + 1)
                    act.activation(SGZ[:, :, :], SGZ[:, :, :], ACT.Ln, bias=1.0).then_inc(sgz_chain, 1)
                if main and s == 15:
                    act.wait_ge(sgz_chain, 2 * J + 2)
                    act.activation(SGZ[:, :, :], SGZ[:, :, :], ACT.Exp, scale=-1.0).then_inc(sgz_ready, 1)

            def first_main():
                act.wait_ge(dt_ready, 1)
                decay(0, 0, 0, 0, 0)
                act.wait_ge(st_ready, 1)
                act.activation(CS[:, 0], ST[:, 0:T], ACT.Copy).then_inc(st_copied, 1)
                decay(0, 0, 0, 0, 1)

            run_units(act, step, first_main)

            act.wait_ge(f_dve, 1)
            act.activation(x0s, x0, ACT.Square).then_inc(f_act, 1)
            act.wait_ge(f_pe, 2)
            act.activation(r0, PP[:, 0, 4:8], ACT.Ln, bias=EPST[:, 0:1]).then_inc(f_act, 1)
            act.wait_ge(f_act, 2)
            act.activation(r0, r0, ACT.Exp, scale=-0.5).then_inc(f_act, 1)
            act.wait_ge(f_dve, 5)
            act.activation(WEX, TOP, ACT.Exp, bias=NMX, accum_out=WSUM).then_inc(f_act, 1)

        @block.tensor
        def _(pe):
            pe.wait_ge(const_ready, 7 + BATCH + 2)
            pe.wait_ge(w_loaded, 16 * N_WLOADS)
            pe.wait_ge(set_dve, 1)
            for h in range(HALVES):
                for k in range(TAPS):
                    last = pe.transpose(Yp[:, h, k * P:(k + 1) * P], WSC[:, h * TAPS + k], IDENT[:, :])
            last.then_inc(set_pe, 1)
            for h in range(HALVES):
                pe.transpose(PP[:, 0, h * P:(h + 1) * P], WNAT[:, HALVES + h], IDENT[:, :])
                pe.transpose(PP[:, 0, 256 + h * P:256 + (h + 1) * P], OPNAT[:, h * P:(h + 1) * P], IDENT[:, :])
                pe.transpose(PP[:, 1, h * 40:h * 40 + 40], XPNAT[:, h * P:(h + 1) * P], IDENT[0:40, 0:40])
                last = pe.transpose(PP[0:XROWS + 1, 1, 128 + h * P:256 + h * P], DTNAT[:, h], IDENT[:, :])
            last.then_inc(set_pe, 1)
            pe.wait_ge(set_act, 4)
            for h in range(HALVES):
                last = pe.matmul(DA[:, 0, h:h + 1], WT[:, h, TAPS - 1], TKC, start=True, stop=True)
            last.then_inc(set_pe, 1)
            pe.wait_ge(set_dve, 5)
            for h in range(HALVES):
                pe.matmul(DA[0:XROWS, 0, 8:9], XPT[:, h, :], TU[:, h:h + 1], start=h == 0, stop=h == 1)
            for h in range(HALVES):
                last = pe.matmul(DA[:, 0, 16:32], UB[:, h], XPT[:, h, 0:NS], start=h == 0, stop=h == 1)
            last.then_inc(set_pe, 1)
            pe.wait_ge(set_act, 8)
            for h in range(HALVES):
                last = pe.matmul(DA[:, 0, 40 + h:41 + h], DTW[DTROW:XROWS + 1, h], XDT[DTROW:XROWS + 1, 0:1],
                                 start=True, stop=True, tile_position=(DTROW, 0))
            last.then_inc(set_pe, 1)

            def spread_b(unit, par, n):
                before = NDVE * unit + dve_index(n)
                positive(pe, dbu_dve, before)
                pe.matmul(BB[:, 0:T], SEL[:, n], PT[:, par], start=True, stop=True).then_inc(b_ready, 1)

            def spread_b_pool(unit, par, n):
                pe.wait_ge(st_copied, STAGES_PER_UNIT * unit + stage_index("B", n))
                pe.matmul(ST[:, 0:T], SEL[:, n], PT[:, par], start=True, stop=True).then_inc(st_ready, 1)

            def spread_c(unit, par, n):
                positive(pe, st_copied, STAGES_PER_UNIT * unit + stage_index("C", n))
                pe.matmul(ST[:, 0:T], SEL[:, NS + n], PT[:, par], start=True, stop=True).then_inc(st_ready, 1)

            def step(J, par, s, main, front, back, prev, conv, norm):
                f, k, g, N = J + 1, J - 1, J + 3, NS * J + s
                fp = kp = 1 - par
                if main:
                    if s + 2 < NS and s + 2 not in POOL_STATES:
                        spread_b(J, par, s + 2)
                    elif s + 2 >= NS and front:
                        spread_b(J + 1, 1 - par, s + 2 - NS)
                if main and s >= LAG or prev and s < LAG:
                    n3 = (s - LAG) % NS
                    pe.wait_ge(m_ready, N - LAG + 1)
                    if s == LAG:
                        positive(pe, v_ready, J)
                    for h in range(HALVES):
                        last = pe.matmul(Yp[:, h, 0:T], IDENT[:, :], M[:, n3 % MRING, h],
                                         start=n3 == 0, stop=n3 == NS - 1)
                    last.then_inc(ysum_done, 1)
                if main and s == 7:
                    for h in range(HALVES):
                        pe.matmul(Yp[:, h, 0:T], DD[:, h], U[:, par, h], start=False, stop=False)
                if front and s == 3:
                    pe.wait_ge(u_ready, f + 1)
                    for h in range(HALVES):
                        last = pe.matmul(PP[0:XROWS, 1, 0:T], XPT[:, h], U[:, fp, h], start=h == 0, stop=h == 1)
                    last.then_inc(xp_ready, 1)
                if back and s == 4:
                    pe.wait_ge(v_ready, k + 1)
                    if front:
                        pe.wait_ge(clamped, 2 * f + 1)
                    for h in range(HALVES):
                        last = pe.matmul(PP[:, 0, 0:T], OPT[:, h], VV[:, h], start=h == 0, stop=h == 1)
                    last.then_inc(op_ready, 1)
                if front and s == 7:
                    pe.wait_ge(hi_ready, f + 1)
                    if back:
                        pe.wait_ge(x2_ready, k + 1)
                    for h in range(HALVES):
                        if h == 1:
                            pe.wait_ge(parts_ready, f + 1)
                        last = pe.matmul(PP[:, h, 0:T], DTW[DTROW:XROWS + 1, h], XDT[DTROW:XROWS + 1, :],
                                         start=True, stop=True, tile_position=(DTROW, 0))
                    last.then_inc(dtp_ready, 1)
                if back and s == 9:
                    pe.wait_ge(x2_ready, k + 1)
                    if front:
                        pe.wait_ge(relu_done, f + 1)
                    for q in range(Q):
                        last = pe.matmul(STAT2, MEANW[:, :], unit_x(k)[:, q], start=q == 0, stop=q == Q - 1)
                    last.then_inc(mean2_ready, 1)
                if main and s == 10:
                    if back:
                        pe.wait_ge(xc2_ready, k + 1)
                    elif front:
                        pe.wait_ge(relu_done, f + 1)
                    if norm:
                        pe.wait_ge(xc_ready, g + 1)
                    for h in range(HALVES):
                        last = pe.matmul(PP[:, h, 0:T], WZT[:, h], unit_seq(J), start=True, stop=True)
                    last.then_inc(z_ready, 1)
                if norm and s == 9:
                    if isinstance(g, int) and g < BATCH:
                        pe.wait_ge(x_first[g], 16)
                    else:
                        pe.wait_ge(x_loaded, 16 * (UNITS - BATCH))
                    if front:
                        pe.wait_ge(relu_done, f + 1)
                    positive(pe, ln_done, g)
                    for q in range(Q):
                        last = pe.matmul(STAT, MEANW[:, :], unit_x(g)[:, q], start=q == 0, stop=q == Q - 1)
                    last.then_inc(mean_ready, 1)
                if back and s == 12:
                    if main:
                        pe.wait_ge(z_clamped, J + 1)
                    pe.wait_ge(sq2_ready, k + 1)
                    for q in range(Q):
                        last = pe.matmul(STAT2, MEANW[:, :], SQ2[:, q], start=q == 0, stop=q == Q - 1)
                    last.then_inc(var2_ready, 1)
                if norm and s == 12:
                    if main:
                        pe.wait_ge(z_clamped, J + 1)
                    pe.wait_ge(sq_ready, g + 1)
                    for q in range(Q):
                        last = pe.matmul(STAT, MEANW[:, :], SQ[:, q], start=q == 0, stop=q == Q - 1)
                    last.then_inc(var_ready, 1)
                if conv and s >= 13:
                    if s == 13:
                        pe.wait_ge(xn_ready, J + 3)
                        if back:
                            pe.wait_ge(ln2_done, k + 1)
                        elif main:
                            pe.wait_ge(z_clamped, J + 1)
                        elif front:
                            pe.wait_ge(relu_done, f + 1)
                    for m in range((s - 13) * 3, min((s - 13) * 3 + 3, HALVES * TAPS)):
                        h, tap = m // TAPS, m % TAPS
                        if m == TAPS:
                            if norm:
                                pe.wait_ge(ln_done, g + 1)
                            else:
                                pe.wait_ge(z_clamped, J + 1)
                        last = pe.matmul(PP[:, h, 0:T], WT[:, h, tap], XN[:, ds((J + 2) * SLOT + tap, T)],
                                         start=tap == 0, stop=tap == TAPS - 1)
                        if tap == TAPS - 1:
                            last.then_inc(conv_ready, 1)
                if main and s + 3 in POOL_STATES:
                    spread_b_pool(J, par, s + 3)
                if main and s < NS - 2:
                    spread_c(J, par, s + 2)
                elif main and front:
                    spread_c(J + 1, 1 - par, s + 2 - NS)

            def first_main():
                pe.wait_ge(parts_ready, 1)
                spread_b(0, 0, 0)
                spread_c(0, 0, 0)
                spread_c(0, 0, 1)
                spread_b(0, 0, 1)

            run_units(pe, step, first_main)

            X0v = X[:, 0:BATCH * T].rearrange("p (b q t) -> p q b t", b=BATCH, q=Q)[:, :, :, 0]
            pe.wait_ge(out_ready, UNITS)
            for q in range(Q):
                last = pe.matmul(PP[:, 0, 0:4], MEANW[:, :], X0v[:, q], start=q == 0, stop=q == Q - 1)
            last.then_inc(f_pe, 1)
            pe.wait_ge(f_act, 1)
            for q in range(Q):
                last = pe.matmul(PP[:, 0, 4:8], MEANW[:, :], x0s[:, q], start=q == 0, stop=q == Q - 1)
            last.then_inc(f_pe, 1)
            pe.wait_ge(f_dve, 2)
            for q in range(Q):
                last = pe.matmul(PP[0:BATCH, 1, 0:MEM], x0[:, q], RW[:, q], start=q == 0, stop=q == Q - 1)
            last.then_inc(f_pe, 1)
            pe.wait_ge(f_dve, 8)
            pe.matmul(PP[:, 0, 16:48], ONE4[:, :], WDG.rearrange("p b k -> p (b k)"), start=True, stop=True)\
                .then_inc(f_pe, 1)
            pe.wait_ge(f_dve, 10)
            for b in range(BATCH):
                pe.wait_ge(g_loaded[b], 16 * TOPK)
                for q in range(Q):
                    for k in range(TOPK):
                        last = pe.matmul((Yp[:, b % 2] if b < 2 else DA[:, b % 2])[:, q * P:(q + 1) * P],
                                         G[:, (b % 2) * TOPK + k].rearrange("p (c q) -> p q c", q=Q)[:, q],
                                         WI[:, b * TOPK + k], start=k == 0, stop=k == TOPK - 1)
                last.then_inc(g_used, 1)

        @block.vector
        def _(dve):
            dve.wait_ge(w_loaded, 16 * N_WLOADS)
            for h in range(HALVES):
                for k in range(TAPS):
                    last = dve.tensor_scalar(WSC[:, h * TAPS + k], WNAT[:, h], CW[:, h, k:k + 1], None, ALU.mult)
            last.then_inc(set_dve, 1)
            dve.wait_ge(const_ready, 7 + BATCH + 1)
            for h in range(HALVES):
                dve.tensor_scalar(DD[:, h], IDENT[:, :], DV[:, h:h + 1], None, ALU.mult)
            dve.memset(LESS[:, :], 0.0).then_inc(less_set, 1)
            dve.wait_ge(less_set, 1)
            dve.memset(LESS[BC:2 * BC, 0:1], -1.0)
            dve.memset(LESS[2 * BC:3 * BC, :], -1.0).then_inc(less_set, 1)
            dve.wait_ge(less_set, 2)
            dve.wait_ge(set_pe, 3)
            dve.tensor_tensor(TUC, DA[:, 0, 0:2], CB_[:, :], ALU.add).then_inc(set_dve, 1)
            dve.wait_ge(set_dve, 2)
            dve.tensor_scalar(TUC, TUC, NEG_LIMIT, None, ALU.max).then_inc(set_dve, 1)
            dve.wait_ge(set_act, 7)
            dve.tensor_tensor(TU, TUC, TSG, ALU.mult).then_inc(set_dve, 1)
            dve.wait_ge(set_dve, 4)
            dve.tensor_copy(UB, TU.unsqueeze(2).broadcast_to([P, HALVES, P])).then_inc(set_dve, 1)
            dve.wait_ge(set_act, 12)
            dve.tensor_tensor(TL, TL, TR, ALU.mult).then_inc(set_dve, 1)
            dve.wait_ge(set_act, 14)
            dve.scalar_tensor_tensor(out=TL, in0=TR, scalar=LOG_D, in1=TL, op0=ALU.add, op1=ALU.mult)\
                .then_inc(set_dve, 1)
            dve.wait_ge(set_dve, 7)
            dve.scalar_tensor_tensor(out=TL, in0=TS, scalar=LOG_H, in1=TL, op0=ALU.add, op1=ALU.mult)\
                .then_inc(set_dve, 1)
            dve.wait_ge(set_pe, 5)
            dve.wait_ge(set_dve, 8)
            dve.scalar_tensor_tensor(out=TDT, in0=DA[:, 0, 40:42], scalar=0.0, in1=TL, op0=ALU.max, op1=ALU.add)\
                .then_inc(set_dve, 1)
            dve.wait_ge(set_dve, 9)
            dve.tensor_tensor(TDU, TDT, TU, ALU.mult).then_inc(set_dve, 1)
            dve.wait_ge(set_dve, 10)
            for h in range(HALVES):
                last = dve.tensor_scalar(CAR[:, 0:NS * HALVES].rearrange("p (n h) -> p n h", h=HALVES)[:, :, h],
                                         DA[:, 0, 16:32], TDU[:, h:h + 1], None, ALU.mult)
            last.then_inc(set_dve, 1)
            dve.wait_ge(set_dve, 11)
            dve.tensor_copy(CAR[:, NS * HALVES:BATCH * NS * HALVES].rearrange("p (b n) -> p b n", b=BATCH - 1),
                            CAR[:, 0:NS * HALVES].unsqueeze(1).broadcast_to([P, BATCH - 1, NS * HALVES]))\
                .then_inc(car_saved, 4 * BATCH)

            def drive(unit, par, n, N):
                positive(dve, m_ready, N - HRING + 1)
                dve.wait_ge(b_ready, NDVE * unit + dve_index(n) + 1)
                dve.tensor_tensor(HB[:, n % HRING], DTU[:, par], over_halves(BB[:, 0:T]), ALU.mult)\
                    .then_inc(dbu_dve, 1)

            def step(J, par, s, main, front, back, prev, conv, norm):
                f, k, g, N = J + 1, J - 1, J + 3, NS * J + s
                fp = kp = 1 - par
                if back and s == 1:
                    dve.wait_ge(sgz_ready, k + 1)
                    dve.tensor_tensor(GZ[:, :, :], GZ[:, :, :], SGZ[:, :, :], ALU.mult).then_inc(gz_ready, 1)
                if back and s == LAG:
                    dve.wait_ge(ysum_done, NS * (k + 1))
                    dve.wait_ge(gz_ready, k + 1)
                    positive(dve, op_ready, k)
                    dve.tensor_tensor(VV[:, :, :], Yp[:, :, 0:T], GZ[:, :, :], ALU.mult).then_inc(v_ready, 1)
                if s % GRP == 1 and (main and s > 1 or prev and s == 1):
                    grp = (s // GRP - 1) % GRP
                    unit = J if s > 1 else J - 1
                    dve.wait_ge(scan_done, 2 * (N - 1))
                    dve.tensor_copy(CAR[:, ds((unit + BATCH) * NS * HALVES + grp * GRP * HALVES, GRP * HALVES)]
                                    .rearrange("p (n h) -> p n h", h=HALVES),
                                    HB[:, (grp % 2) * GRP:(grp % 2) * GRP + GRP, :, T - 1]).then_inc(car_saved, 1)
                if main:
                    if s + 1 < NS and s + 1 not in POOL_STATES:
                        drive(J, par, s + 1, N + 1)
                    elif s + 1 == NS and front:
                        dve.wait_ge(dtu_ready, J + 2)
                        drive(J + 1, 1 - par, 0, N + 1)
                if front and s == 6:
                    dve.wait_ge(hi_ready, f + 1)
                    dve.scalar_tensor_tensor(out=PP[0:DTROW, 1, 0:T], in0=PART[:, :], scalar=LESS[:, 0:1],
                                             in1=PP[0:DTROW, 1, 0:T], op0=ALU.mult, op1=ALU.add)\
                        .then_inc(res_ready, 1)
                if back and s == 10:
                    dve.wait_ge(mean2_ready, k + 1)
                    positive(dve, out_ready, k)
                    dve.tensor_tensor(XC2[:, :, :], unit_x(k), over_q(STAT2), ALU.subtract).then_inc(xc2_ready, 1)
                if norm and s == 10:
                    dve.wait_ge(mean_ready, g + 1)
                    positive(dve, xn_ready, g)
                    dve.tensor_tensor(XC[:, :, :], unit_x(g), over_q(STAT), ALU.subtract).then_inc(xc_ready, 1)
                if front and s == 13:
                    dve.wait_ge(r2_ready, 2 * f + 1)
                    dve.scalar_tensor_tensor(out=SE[:, :, :], in0=SR[:, :, :], scalar=LOG_D, in1=SE[:, :, :],
                                             op0=ALU.add, op1=ALU.mult).then_inc(m1_done, 1)
                if front and s == 3:
                    dve.wait_ge(clamped, 2 * f + 2)
                    dve.wait_ge(sg_ready, f + 1)
                    dve.tensor_tensor(U[:, fp], U[:, fp], SG[:, :, :], ALU.mult).then_inc(u_ready, 1)
                if main:
                    if s in POOL_STATES:
                        dve.wait_ge(dbu_pool, NPOOL * J + pool_index(s) + 1)
                    else:
                        dve.wait_ge(dbu_dve, NDVE * J + dve_index(s) + 1)
                    dve.wait_ge(car_saved, 4 * J + s // GRP + 1)
                    for h in range(HALVES):
                        dve.wait_ge(da_ready, 2 * N + h + 1)
                        dve.tensor_tensor_scan(HB[:, s % HRING, h], DA[:, h, 0:T], HB[:, s % HRING, h],
                                               CAR[:, ds(J * NS * HALVES + s * HALVES + h, 1)],
                                               ALU.mult, ALU.add).then_inc(scan_done, 1)
                if front and s == 0:
                    for h in range(HALVES):
                        dve.wait_ge(conv_ready, 2 * f + h + 1)
                        dve.tensor_scalar(U[:, fp, h], PP[:, h, 0:T], CB_[:, h:h + 1], NEG_LIMIT, ALU.add, ALU.max)\
                            .then_inc(clamped, 1)
                if back and s == 5:
                    dve.wait_ge(op_ready, k + 1)
                    for r1 in range(2):
                        xr = by_row_parity(unit_x(k), r1)
                        last = dve.tensor_tensor(xr, xr, seq_rows(PP[:, 0, 0:T], r1), ALU.add)
                    last.then_inc(x2_ready, 1)
                if front and s == 6:
                    dve.wait_ge(mid_ready, f + 1)
                    dve.scalar_tensor_tensor(out=PT[:, fp], in0=PART[:, :], scalar=LESS[:, 1:2],
                                             in1=PP[0:DTROW, 1, 0:T], op0=ALU.mult, op1=ALU.add)\
                        .then_inc(parts_ready, 1)
                if main and s == 11:
                    dve.wait_ge(z_ready, J + 1)
                    if back:
                        dve.wait_ge(v_ready, k + 1)
                    dve.tensor_scalar(GZ[:, :, :], PPT, NEG_LIMIT, None, ALU.max).then_inc(z_clamped, 1)
                if front and s == 13:
                    dve.wait_ge(r2_ready, 2 * f + 2)
                    dve.wait_ge(m1_done, 2 * f + 1)
                    dve.scalar_tensor_tensor(out=SE[:, :, :], in0=SS[:, :, :], scalar=LOG_H, in1=SE[:, :, :],
                                             op0=ALU.add, op1=ALU.mult).then_inc(m1_done, 1)
                    dve.wait_ge(relu_done, f + 1)
                    dve.wait_ge(m1_done, 2 * f + 2)
                    dve.tensor_tensor(DT[:, fp], DT[:, fp], SE[:, :, :], ALU.add).then_inc(dt_ready, 1)

            def first_main():
                dve.wait_ge(dtu_ready, 1)
                drive(0, 0, 0, 0)

            run_units(dve, step, first_main)

            X0v = X[:, 0:BATCH * T].rearrange("p (b q t) -> p q b t", b=BATCH, q=Q)[:, :, :, 0]
            dve.wait_ge(f_pe, 1)
            dve.tensor_tensor(x0, X0v, PP[:, 0, 0:4].unsqueeze(1).broadcast_to([P, Q, BATCH]), ALU.subtract)\
                .then_inc(f_dve, 1)
            dve.wait_ge(f_act, 3)
            dve.tensor_tensor(x0, x0, r0.unsqueeze(1).broadcast_to([P, Q, BATCH]), ALU.mult).then_inc(f_dve, 1)
            dve.wait_ge(f_pe, 3)
            dve.tensor_copy(SCO, PP[0:BATCH, 1, 0:MEM]).then_inc(f_dve, 1)
            dve.wait_ge(f_dve, 3)
            dve.max(TOP, SCO).then_inc(f_dve, 1)
            dve.wait_ge(f_dve, 4)
            dve.tensor_scalar(NMX, TOP[:, 0:1], -1.0, None, ALU.mult).then_inc(f_dve, 1)
            dve.max_index(IDX[:, :], TOP, SCO).then_inc(idx_ready, 1)
            dve.wait_ge(f_act, 4)
            dve.reciprocal(WRC, WSUM).then_inc(f_dve, 1)
            dve.wait_ge(f_dve, 6)
            dve.tensor_scalar(WNM, WEX, WRC, None, ALU.mult).then_inc(f_dve, 1)
            dve.wait_ge(f_dve, 7)
            dve.tensor_tensor(WDG, IDENT[0:BATCH, 0:BATCH].unsqueeze(2).broadcast_to([BATCH, BATCH, TOPK]),
                              WNM.unsqueeze(1).broadcast_to([BATCH, BATCH, TOPK]), ALU.mult).then_inc(f_dve, 1)
            dve.wait_ge(f_pe, 4)
            dve.tensor_copy(WBC, PP[:, 0, 16:48]).then_inc(f_dve, 1)
            dve.wait_ge(f_dve, 9)
            dve.tensor_tensor(WI, IDENT[:, :].unsqueeze(1).broadcast_to([P, BATCH * TOPK, P]),
                              WBC.unsqueeze(2).broadcast_to([P, BATCH * TOPK, P]), ALU.mult).then_inc(f_dve, 1)
            for b in range(BATCH):
                ps = (Yp[:, b % 2] if b < 2 else DA[:, b % 2]).rearrange("p (q t) -> p q t", q=Q)
                dve.wait_ge(g_used, b + 1)
                o0 = unit_seq(b).rearrange("p (q t) -> p q t", q=Q)
                o1 = unit_seq(BATCH + b).rearrange("p (q t) -> p q t", q=Q)
                dve.tensor_tensor(o0[:, :, 1:TOK], unit_x(b)[:, :, 1:TOK], ps[:, :, 0:TOK - 1], ALU.add)
                rest = MT - (TOK - 1)
                dve.tensor_tensor(o1[:, :, 0:rest], unit_x(BATCH + b)[:, :, 0:rest], ps[:, :, TOK - 1:MT], ALU.add)\
                    .then_inc(comb_done, 1)


_NAMES = ["x", "L0_conv_global_token", "L0_conv_in_proj_w", "L0_conv_conv_w", "L0_conv_conv_b",
          "L0_conv_x_proj_w", "L0_conv_dt_proj_w", "L0_conv_dt_proj_b", "L0_conv_A_log", "L0_conv_D",
          "L0_conv_out_proj_w", "L0_ffn_memory_tokens", "L0_ffn_memory_router"]


def kernel(**inputs):
    import numpy as np
    import concourse.bacc as bacc
    from concourse.bass_utils import run_bass_kernel_spmd as run

    nc = bacc.Bacc("TRN2", target_bir_lowering=False, num_devices=1)
    arrays, args = {}, []
    for name in _NAMES:
        a = np.ascontiguousarray(inputs[name])
        arrays[f"in_{name}"] = a
        args.append(nc.dram_tensor(f"in_{name}", a.shape, mybir.dt.from_np(a.dtype), kind="ExternalInput").ap())
    shape = inputs["x"].shape
    result = nc.dram_tensor("out_0", shape, F32, kind="ExternalOutput").ap()
    build(nc, *args, result)
    r = run(nc, [arrays], core_ids=[0])
    return r.results[0]["out_0"]
```

```python
from contextlib import ExitStack

import concourse.bass as bass
from concourse import mybir
from concourse.bass import ds

F32 = mybir.dt.float32
BF16 = mybir.dt.bfloat16
U32 = mybir.dt.uint32
ACT = mybir.ActivationFunctionType
ALU = mybir.AluOpType

P = 128
BATCH, DIM, HH, WW = 4, 512, 24, 24
Q = DIM // P
HALVES = 2
NS = 16
RANK = 8
TAPS = 4
HIST = TAPS - 1
ROWS = 4
CHUNKS = HH // ROWS
TOK = ROWS * WW
T = TOK * Q
UNITS = CHUNKS * BATCH
SLOT = HIST + T
TOPK = 8
MEM, MT = 256, 128
BC = 2 * NS
PARTS = 3
DTROW = PARTS * BC
XROWS = DTROW + RANK
XP_M = XROWS
NEG_LIMIT = -44.0
EPS_C, EPS_T = 1e-6, 1e-5
LOG_C, LOG_D, LOG_G, LOG_H = 0.34222454, 1.83313539, 0.33814541, 1.75319741 ** 2
POOL_STATES = (3, 5, 7, 9)
NPOOL = len(POOL_STATES)
NDVE = NS - NPOOL
HRING, MRING, CRING = 8, 4, 4
LAG = 3
GRP = 4

STAGES_PER_UNIT = NS + NPOOL


def dve_index(n):
    return sum(1 for m in range(n) if m not in POOL_STATES)


def pool_index(n):
    return POOL_STATES.index(n)


def staged(s):
    return [("B", s + 3)] * (s + 3 in POOL_STATES) + [("C", s + 2)]


def stage_index(kind, n):
    order = [("C", 0), ("C", 1)] + [use for s in range(NS - 2) for use in staged(s)]
    return order.index((kind, n))


def build(nc, x, tok, w_in, conv_w, conv_b, xp_w, dt_w, dt_b, a_log, dvec, op_w, mem, router, out):
    ctx = ExitStack()
    with ctx:
        def sb(name, shape, dt=F32):
            return ctx.enter_context(nc.sbuf_tensor(name, shape, dt))

        def sem(name):
            return ctx.enter_context(nc.semaphore(name))

        X = sb("X", [P, UNITS * T])
        XN = sb("XN", [P, (UNITS + BATCH) * SLOT])
        CAR = sb("CAR", [P, (UNITS + BATCH) * NS * HALVES])
        SCAN = sb("SCAN", [P, (HRING + MRING) * HALVES * T])
        HB = SCAN[:, 0:HRING * HALVES * T].rearrange("p (r h t) -> p r h t", r=HRING, h=HALVES)
        M = SCAN[:, HRING * HALVES * T:].rearrange("p (r h t) -> p r h t", r=MRING, h=HALVES)
        UDT = sb("UDT", [P, 6 * HALVES * T])
        UDTv = UDT[:, :].rearrange("p (k r h t) -> p k r h t", k=3, r=2, h=HALVES)
        U, DT, DTU = (UDTv[:, k] for k in range(3))
        CS = sb("CS", [P, CRING, T])
        BS = sb("BS", [P, 2, T])
        XC = sb("XC", [P, Q, TOK]); SQ = sb("SQ", [P, Q, TOK])
        LNV = sb("LNV", [P, TOK]); RSTD = sb("RSTD", [P, TOK])
        XC2 = sb("XC2", [P, Q, TOK]); SQ2 = sb("SQ2", [P, Q, TOK])
        LNV2 = sb("LNV2", [P, TOK]); RSTD2 = sb("RSTD2", [P, TOK])
        GATES = sb("GATES", [P, 4 * HALVES * T])
        SG, SE, SR, SS = (GATES[:, i * HALVES * T:(i + 1) * HALVES * T].rearrange("p (h t) -> p h t", h=HALVES)
                          for i in range(4))
        SGZ = sb("SGZ", [P, HALVES, T])
        GZ = sb("GZ", [P, HALVES, T])
        VV = sb("VV", [P, HALVES, T])
        PT = sb("PT", [DTROW, 2, T], BF16)
        PART = sb("PART", [DTROW, T], BF16)
        LESS = sb("LESS", [DTROW, PARTS - 1])
        XDT0 = sb("XDT0", [P, 1])
        XDT = sb("XDT", [P, T])
        WT = sb("WT", [P, HALVES, TAPS, P])
        WZT = sb("WZT", [P, HALVES, P])
        XPT = sb("XPT", [P, HALVES, XP_M])
        DTW = sb("DTW", [P, HALVES, P])
        OPT = sb("OPT", [P, HALVES, P])
        DD = sb("DD", [P, HALVES, P])
        IDENT = sb("IDENT", [P, P]); MEANW = sb("MEANW", [P, P])
        SEL = sb("SEL", [DTROW, BC, P], BF16)
        A = sb("A", [P, HALVES, NS]); AE = sb("AE", [P, HALVES, NS])
        CB_ = sb("conv_bias", [P, HALVES]); DV = sb("DV", [P, HALVES])
        CW = sb("CW", [P, HALVES, TAPS])
        EPSC = sb("EPSC", [P, 1]); EPST = sb("EPST", [P, 1])
        LOGB = sb("LOGB", [P, 2])
        RW = sb("RW", [P, Q, MEM])
        WNAT = SCAN[:, 0:512].rearrange("p (k c) -> p k c", k=4)
        WSC = SCAN[:, 512:1536].rearrange("p (k c) -> p k c", k=8)
        OPNAT = SCAN[:, 1536:1792]
        XPNAT = SCAN[0:RANK + BC, 1792:2048]
        DTNAT = SCAN[:, 2048:2048 + 2 * (XROWS + 1)].rearrange("p (k c) -> p k c", k=2)
        TKC = SCAN[:, 2304:2305]
        TU = SCAN[:, 2306:2308]; TSG = SCAN[:, 2308:2310]; TUC = SCAN[:, 2310:2312]
        TL = SCAN[:, 2312:2314]; TR = SCAN[:, 2576:2578]; TS = SCAN[:, 2578:2580]; TDT = SCAN[:, 2314:2316]; TDU = SCAN[:, 2316:2318]
        UB = SCAN[:, 2320:2576].rearrange("p (k c) -> p k c", k=2)
        G = [buf[:, 2 * BATCH * slot:2 * BATCH * slot + TOPK * DIM].rearrange("p (k d) -> p k d", k=TOPK)
             for buf, slot in ((X, T), (XN, SLOT))]
        WI = GATES[:, :].rearrange("p (b k t) -> p b k t", b=BATCH - 1, t=P)
        small = SQ[:, :, :].rearrange("p q t -> p (q t)")
        x0 = small[:, 0:16].rearrange("p (q b) -> p q b", q=Q)
        x0s = small[:, 16:32].rearrange("p (q b) -> p q b", q=Q)
        r0 = small[:, 32:36]
        WBC = small[:, 40:72]
        TOP = small[0:BATCH, 80:88]
        NMX = small[0:BATCH, 88:89]
        WEX = small[0:BATCH, 96:104]
        WSUM = small[0:BATCH, 104:105]
        WRC = small[0:BATCH, 105:106]
        WNM = small[0:BATCH, 112:120]
        WDG = small[0:BATCH, 120:152].rearrange("p (b k) -> p b k", b=BATCH)
        SCO = XC[0:BATCH, :, :].rearrange("p q t -> p (q t)")[:, 0:MEM]
        IDX = sb("IDX", [BATCH, TOPK], U32)
        ONE4 = sb("ONE4", [BATCH, P])

        Yp = ctx.enter_context(nc.psum_tensor("Yp", [P, HALVES, 512], F32))
        DA = ctx.enter_context(nc.psum_tensor("DA", [P, HALVES, 512], F32))
        BB = ctx.enter_context(nc.psum_tensor("BB", [P, 512], F32))
        ST = ctx.enter_context(nc.psum_tensor("ST", [P, 512], F32))
        PP = ctx.enter_context(nc.psum_tensor("PP", [P, HALVES, 512], F32))
        STAT = PP[:, 1, 0:TOK]; STAT2 = PP[:, 0, 0:TOK]
        PPT = PP[:, :, 0:T]

        w_loaded = sem("w_loaded"); wc_loaded = sem("wc_loaded"); x_loaded = sem("x_loaded")
        x_first = [sem(f"x_first{b}") for b in range(BATCH)]
        ffn_loaded = sem("ffn_loaded")
        const_ready = sem("const_ready")
        zeroed = sem("zeroed"); ident_ready = sem("ident_ready"); sel_ready = sem("sel_ready")
        less_set = sem("less_set")
        set_pe = sem("set_pe"); set_act = sem("set_act"); set_dve = sem("set_dve")
        mean_ready = sem("mean_ready"); xc_ready = sem("xc_ready"); sq_ready = sem("sq_ready")
        var_ready = sem("var_ready"); ln_done = sem("ln_done"); rstd_ready = sem("rstd_ready")
        xn_part = sem("xn_part"); xn_ready = sem("xn_ready")
        conv_ready = sem("conv_ready"); clamped = sem("clamped"); sg_chain = sem("sg_chain")
        sg_ready = sem("sg_ready"); u_ready = sem("u_ready"); xp_ready = sem("xp_ready")
        hi_ready = sem("hi_ready"); res_ready = sem("res_ready"); mid_ready = sem("mid_ready")
        parts_ready = sem("parts_ready"); dtp_ready = sem("dtp_ready"); sp_chain = sem("sp_chain")
        relu_done = sem("relu_done"); sq_e_ready = sem("sq_e_ready"); cr_ready = sem("cr_ready"); r2_ready = sem("r2_ready"); m1_done = sem("m1_done"); dt_ready = sem("dt_ready"); dtu_ready = sem("dtu_ready")
        b_ready = sem("b_ready"); dbu_dve = sem("dbu_dve"); dbu_pool = sem("dbu_pool")
        st_ready = sem("st_ready"); st_copied = sem("st_copied")
        da_ready = sem("da_ready"); scan_done = sem("scan_done"); car_saved = sem("car_saved")
        m_ready = sem("m_ready"); ysum_done = sem("ysum_done")
        z_ready = sem("z_ready"); z_clamped = sem("z_clamped"); sgz_chain = sem("sgz_chain")
        sgz_ready = sem("sgz_ready"); gz_ready = sem("gz_ready"); v_ready = sem("v_ready")
        op_ready = sem("op_ready"); x2_ready = sem("x2_ready")
        mean2_ready = sem("mean2_ready"); xc2_ready = sem("xc2_ready"); sq2_ready = sem("sq2_ready")
        var2_ready = sem("var2_ready"); ln2_done = sem("ln2_done"); rstd2_ready = sem("rstd2_ready")
        xh2_done = sem("xh2_done"); out_ready = sem("out_ready"); stored = sem("stored")
        f_pe = sem("f_pe"); f_act = sem("f_act"); f_dve = sem("f_dve")
        idx_ready = sem("idx_ready"); g_loaded = [sem(f"g_loaded{b}") for b in range(BATCH)]
        g_used = sem("g_used"); comb_done = sem("comb_done")

        N_WLOADS = 8
        block = ctx.enter_context(nc.Block())
        ROUTE = UNITS - 3
        COMB = UNITS - 1
        COMBINE = {(COMB, 1 + q): [(0, q)] for q in range(Q)}
        COMBINE.update({(COMB, 6 + q): [(1, q)] for q in range(Q)})
        COMBINE.update({(COMB, 12 + q): [(2, q)] for q in range(Q)})
        COMBINE.update({(COMB + 1, 3): [(3, 0), (3, 1)], (COMB + 1, 5): [(3, 2), (3, 3)]})
        ADD = {(COMB, 5): 0, (COMB, 10): 1, (COMB + 1, 1): 2, (COMB + 1, 13): 3}

        def comb_bank(b):
            return PP[:, 1] if b < 3 else DA[:, 0]

        def unit_x(j):
            return X[:, ds(j * T, T)].rearrange("p (q t) -> p q t", q=Q)

        def unit_seq(j):
            return XN[:, ds(j * SLOT + HIST, T)]

        def by_row_parity(ap_qt, r1):
            return ap_qt[:, 2 * r1:2 * r1 + 2, :].rearrange("p r (h w) -> p h w r", w=WW)

        def seq_rows(ap_t, r1):
            return ap_t.rearrange("p (h r w s) -> p h r w s", h=ROWS, r=2, w=WW)[:, :, r1]

        def over_q(ap):
            return ap.unsqueeze(1).broadcast_to([P, Q, TOK])

        def over_halves(ap):
            return ap.unsqueeze(1).broadcast_to([P, HALVES, T])

        def at(J, unit):
            return isinstance(J, int) and J == unit

        def positive(eng, s, v):
            if isinstance(v, int) and v <= 0:
                return
            assert isinstance(v, int) or v.min_val > 0
            eng.wait_ge(s, v)

        def run_units(eng, step, before_conv=None, before_front=None, first_main=None):
            def unit(J, par, main=True, front=True, back=True, conv=True, norm=True):
                prev = back
                for s in range(NS):
                    step(J, par, s, main, front, back, prev, conv, norm)
            unit(-3, 1, main=False, front=False, back=False, conv=False)
            if before_conv:
                before_conv()
            unit(-2, 0, main=False, front=False, back=False)
            if before_front:
                before_front()
            unit(-1, 1, main=False, back=False)
            if first_main:
                first_main()
            unit(0, 0, back=False)
            unit(1, 1)
            with eng.Fori(1, (UNITS - 4) // 2) as i:
                unit(2 * i, 0)
                unit(2 * i + 1, 1)
            unit(UNITS - 4, 0)
            unit(UNITS - 3, 1, norm=False)
            unit(UNITS - 2, 0, conv=False, norm=False)
            unit(UNITS - 1, 1, front=False, conv=False, norm=False)
            unit(UNITS, 0, main=False, front=False, conv=False, norm=False)

        @block.sync
        def _(sp):
            xv = x.rearrange("b (p q) (c s) w -> c p b q (s w)", q=Q, s=ROWS)
            ov = out.rearrange("b (p q) (c s) w -> c b p q (s w)", q=Q, s=ROWS)
            Xc = X[:, :].rearrange("p (c b q t) -> p c b q t", c=CHUNKS, b=BATCH, q=Q)
            sp.dma_start(CW[:, :, :], conv_w.rearrange("(k e) t -> e k t", e=P)).then_inc(wc_loaded, 16)
            sp.dma_start(WNAT, w_in.rearrange("(k e) c -> e k c", e=P)).then_inc(wc_loaded, 16)
            sp.dma_start(Xc[:, 0, 0], xv[0, :, 0]).then_inc(x_first[0], 16)
            sp.dma_start(OPNAT, op_w).then_inc(w_loaded, 16)
            sp.dma_start(XPNAT, xp_w).then_inc(w_loaded, 16)
            sp.dma_start(CB_[:, :], conv_b.rearrange("(k e) -> e k", e=P), allow_slow_non_contiguous=True).then_inc(w_loaded, 16)
            sp.dma_start(DV[:, :], dvec.rearrange("(k e) -> e k", e=P), allow_slow_non_contiguous=True).then_inc(w_loaded, 16)
            sp.dma_start(AE[:, :, :], a_log.rearrange("(k e) n -> e k n", e=P)).then_inc(w_loaded, 16)
            sp.dma_start(TKC, tok.rearrange("a b c -> c (a b)"), allow_slow_non_contiguous=True).then_inc(w_loaded, 16)
            sp.wait_ge(zeroed, 1)
            sp.dma_start(DTNAT[:, :, DTROW:XROWS],
                         dt_w.rearrange("(k e) r -> e k r", e=P)).then_inc(w_loaded, 16)
            sp.dma_start(DTNAT[:, :, XROWS:XROWS + 1],
                         dt_b.rearrange("(k e r) -> e k r", e=P, r=1), allow_slow_non_contiguous=True).then_inc(w_loaded, 16)
            for b in range(1, BATCH):
                sp.dma_start(Xc[:, 0, b], xv[0, :, b]).then_inc(x_first[b], 16)
            sp.dma_start(RW[:, :, :], router.rearrange("(p q) m -> p q m", q=Q)).then_inc(ffn_loaded, 16)
            for c in range(1, CHUNKS):
                for b in range(BATCH):
                    sp.dma_start(Xc[:, c, b], xv[c, :, b]).then_inc(x_loaded, 16)

            def store(c, b, j):
                sp.wait_ge(out_ready, j + 1)
                sp.dma_start(ov[ds(c, 1), ds(b, 1)].rearrange("c b p q t -> (c b p) q t"),
                             unit_seq(j).rearrange("p (q t) -> p q t", q=Q)).then_inc(stored, 16)
            with sp.Fori(2, CHUNKS - 1) as c:
                with sp.Fori(0, BATCH) as b:
                    store(c, b, c * BATCH + b)
            store(CHUNKS - 1, 0, UNITS - 4)

            def gather(b):
                for k in range(TOPK):
                    m = sp.value_load(IDX[b:b + 1, k:k + 1], min_val=0, max_val=MEM - 1)
                    sp.dma_start(G[b % 2][:, k], mem[ds(m, 1)].rearrange("a t d -> (a t) d"))\
                        .then_inc(g_loaded[b], 16)

            def store_routed(b):
                sp.wait_ge(comb_done, b + 1)
                for c in range(2):
                    sp.dma_start(ov[c, b], unit_seq(c * BATCH + b).rearrange("p (q t) -> p q t", q=Q))\
                        .then_inc(stored, 16)

            sp.wait_ge(idx_ready, 1)
            gather(0)
            sp.wait_ge(stored, 16 * (UNITS - 4 - 2 * BATCH + 1))
            gather(1)
            store(CHUNKS - 1, 1, UNITS - 3)
            sp.wait_ge(g_used, 1)
            gather(2)
            sp.wait_ge(g_used, 2)
            gather(3)
            store_routed(0)
            store_routed(1)
            store(CHUNKS - 1, 2, UNITS - 2)
            store_routed(2)
            store_routed(3)
            store(CHUNKS - 1, 3, UNITS - 1)
            sp.wait_ge(stored, 16 * UNITS)

        @block.gpsimd
        def _(pool):
            pool.memset(DTNAT, 0.0).then_inc(zeroed, 1)
            pool.memset(MEANW[:, :], 1.0 / DIM).then_inc(const_ready, 1)
            pool.memset(IDENT[:, :], 0.0).then_inc(zeroed, 1)
            pool.memset(EPSC[:, :], EPS_C).then_inc(const_ready, 1)
            pool.memset(EPST[:, :], EPS_T).then_inc(const_ready, 1)
            pool.memset(LOGB[:, 0:1], 2.0 / LOG_C).then_inc(const_ready, 1)
            pool.memset(LOGB[:, 1:2], -LOG_G).then_inc(const_ready, 1)
            pool.wait_ge(zeroed, 2)
            pool.affine_select(out=IDENT[:, :], in_=IDENT[:, :], compare_op=ALU.not_equal, fill=1.0,
                               base=0, pattern=[[-1, P]], channel_multiplier=1).then_inc(ident_ready, 1)
            pool.memset(XDT0[:, :], 1.0).then_inc(const_ready, 1)
            pool.memset(XDT[:, :], 1.0).then_inc(const_ready, 1)
            pool.memset(ONE4[:, :], 1.0).then_inc(const_ready, 1)
            for b in range(BATCH):
                pool.memset(XN[:, b * SLOT:b * SLOT + HIST - 1], 0.0).then_inc(const_ready, 1)
            pool.wait_ge(w_loaded, 16 * N_WLOADS)
            for b in range(BATCH):
                pool.tensor_copy(XN[:, b * SLOT + HIST - 1:b * SLOT + HIST], TKC).then_inc(const_ready, 1)

            def selectors():
                pool.memset(SEL[:, :, :], 0.0).then_inc(zeroed, 1)
                for part in range(PARTS):
                    pool.wait_ge(zeroed, 3 + part)
                    pool.affine_select(out=SEL[:, :, :], in_=SEL[:, :, :], compare_op=ALU.not_equal, fill=1.0,
                                       base=-part * BC, pattern=[[-1, BC], [0, P]], channel_multiplier=1)\
                        .then_inc(zeroed if part < PARTS - 1 else sel_ready, 1)

            def step(J, par, s, main, front, back, prev, conv, norm):
                f, k, g, N = J + 1, J - 1, J + 3, NS * J + s
                fp = kp = 1 - par
                if main and (s > 0 or prev) or (s == 0 and prev):
                    n1 = (s - 1) % NS
                    unit1 = J if s else J - 1
                    pool.wait_ge(scan_done, 2 * N)
                    pool.wait_ge(st_copied, STAGES_PER_UNIT * unit1 + stage_index("C", n1) + 1)
                    positive(pool, ysum_done, N - MRING)
                    pool.tensor_tensor(M[:, n1 % MRING], HB[:, n1 % HRING],
                                       over_halves(CS[:, n1 % CRING]), ALU.mult).then_inc(m_ready, 1)
                if main and s + 2 in POOL_STATES:
                    n2 = s + 2
                    pool.wait_ge(st_copied, STAGES_PER_UNIT * J + stage_index("B", n2) + 1)
                    pool.wait_ge(dtu_ready, J + 1)
                    pool.wait_ge(car_saved, 4 * BATCH + 4 * J + (n2 - HRING) // GRP + 1)
                    pool.tensor_tensor(HB[:, n2 % HRING], DTU[:, par], over_halves(BS[:, pool_index(n2) % 2]),
                                       ALU.mult).then_inc(dbu_pool, 1)
                if front and s == 11:
                    pool.wait_ge(sq_e_ready, f + 1)
                    pool.tensor_tensor(SE[:, :, :], SE[:, :, :], SR[:, :, :], ALU.mult).then_inc(cr_ready, 1)
                if back and s == 13:
                    pool.wait_ge(rstd2_ready, k + 1)
                    pool.tensor_tensor(XC2[:, :, :], XC2[:, :, :], over_q(RSTD2[:, :]), ALU.mult)\
                        .then_inc(xh2_done, 1)
                if back and s == 14:
                    pool.wait_ge(xh2_done, k + 1)
                    pool.tensor_tensor(unit_seq(k).rearrange("p (q t) -> p q t", q=Q), XC2[:, :, :], unit_x(k),
                                       ALU.add).then_inc(out_ready, 1)
                if front and s == 13:
                    pool.wait_ge(dt_ready, f + 1)
                    pool.tensor_tensor(DTU[:, fp], DT[:, fp], U[:, fp], ALU.mult).then_inc(dtu_ready, 1)
                if norm and s == 15:
                    pool.wait_ge(rstd_ready, g + 1)
                    for r1 in range(2):
                        pool.tensor_tensor(seq_rows(unit_seq(g), r1), by_row_parity(XC[:, :, :], r1),
                                           by_row_parity(over_q(RSTD[:, :]), r1), ALU.mult).then_inc(xn_part, 1)
                    pool.wait_ge(xn_part, 2 * (g + 1))
                    pool.tensor_copy(XN[:, ds((g + BATCH) * SLOT, HIST)],
                                     XN[:, ds(g * SLOT + T, HIST)]).then_inc(xn_ready, 1)

            run_units(pool, step, before_front=selectors)

        @block.scalar
        def _(act):
            act.preload_act_table_set("natural_log_exp_and_others")
            act.wait_ge(const_ready, 7)

            def weights():
                act.wait_ge(w_loaded, 16 * N_WLOADS)
                act.activation(A[:, :, :], AE[:, :, :], ACT.Exp).then_inc(set_act, 1)
                act.wait_ge(set_act, 1)
                act.activation(A[:, :, :], A[:, :, :], ACT.Copy, scale=-1.0).then_inc(set_act, 1)
                act.wait_ge(set_pe, 1)
                act.activation(WT[:, :, :, :].rearrange("p h k c -> p h (k c)"), Yp[:, :, :], ACT.Copy)\
                    .then_inc(set_act, 1)
                act.wait_ge(set_pe, 2)
                act.activation(WZT[:, :, :].rearrange("p h c -> p (h c)"), PP[:, 0, 0:256], ACT.Copy)
                act.activation(OPT[:, :, :].rearrange("p h c -> p (h c)"), PP[:, 0, 256:512], ACT.Copy)
                for h in range(HALVES):
                    xp = PP[:, 1, h * 40:h * 40 + 40]
                    for part in range(PARTS):
                        act.activation(XPT[:, h, part * BC:(part + 1) * BC], xp[:, RANK:RANK + BC], ACT.Copy)
                    act.activation(XPT[:, h, DTROW:XROWS], xp[:, 0:RANK], ACT.Copy)
                    last = act.activation(DTW[DTROW:XROWS + 1, h], PP[DTROW:XROWS + 1, 1, 128 + h * P:256 + h * P],
                                          ACT.Copy)
                last.then_inc(set_act, 1)

            def decay(J, par, n, N, h):
                positive(act, scan_done, 2 * N - 1 + h)
                act.activation(DA[:, h, 0:T], DT[:, par, h], ACT.Exp, scale=A[:, h, n:n + 1])\
                    .then_inc(da_ready, 1)

            def step(J, par, s, main, front, back, prev, conv, norm):
                f, k, g, N = J + 1, J - 1, J + 3, NS * J + s
                fp = kp = 1 - par
                if front and s == 1:
                    act.wait_ge(clamped, 2 * f + 2)
                    positive(act, u_ready, f)
                    act.activation(SG[:, :, :], U[:, fp], ACT.Exp, scale=-1.0).then_inc(sg_chain, 1)
                if front and s == 6:
                    act.wait_ge(res_ready, f + 1)
                    act.activation(PART[:, :], PP[0:DTROW, 1, 0:T], ACT.Copy).then_inc(mid_ready, 1)
                if front and s == 12:
                    act.wait_ge(cr_ready, f + 1)
                    act.activation(SR[:, :, :], SE[:, :, :], ACT.Square, scale=1.0 / LOG_C).then_inc(r2_ready, 1)
                    act.wait_ge(r2_ready, 2 * f + 1)
                    act.activation(SS[:, :, :], SR[:, :, :], ACT.Square, bias=LOGB[:, 1:2]).then_inc(r2_ready, 1)
                if front and s == 4:
                    act.wait_ge(xp_ready, f + 1)
                    positive(act, parts_ready, f)
                    act.activation(PART[:, :], PP[0:DTROW, 1, 0:T], ACT.Copy)
                    act.activation(XDT[DTROW:XROWS, :], PP[DTROW:XROWS, 1, 0:T], ACT.Copy).then_inc(hi_ready, 1)
                if main:
                    if s < NS - 1:
                        unit, upar, n1 = J, par, s + 1
                    else:
                        unit, upar, n1 = J + 1, 1 - par, 0
                    if s < NS - 1 or front:
                        if n1 == 0:
                            act.wait_ge(dt_ready, unit + 1)
                        decay(unit, upar, n1, N + 1, 0)
                        act.wait_ge(st_ready, STAGES_PER_UNIT * unit + stage_index("C", n1) + 1)
                        positive(act, m_ready, N + 2 - CRING)
                        act.activation(CS[:, n1 % CRING], ST[:, 0:T], ACT.Copy).then_inc(st_copied, 1)
                        decay(unit, upar, n1, N + 1, 1)
                    for n in [n for kind, n in staged(s) if kind == "B"]:
                        act.wait_ge(st_ready, STAGES_PER_UNIT * J + stage_index("B", n) + 1)
                        positive(act, dbu_pool, NPOOL * J + pool_index(n) - 1)
                        act.activation(BS[:, pool_index(n) % 2], ST[:, 0:T], ACT.Copy).then_inc(st_copied, 1)
                if at(J, -1) and s == 1:
                    act.wait_ge(set_dve, 3)
                    act.activation(TSG, TUC, ACT.Exp, scale=-1.0).then_inc(set_act, 1)
                if at(J, -1) and s == 2:
                    act.wait_ge(set_act, 5)
                    act.activation(TSG, TSG, ACT.Ln, bias=1.0).then_inc(set_act, 1)
                    act.wait_ge(set_act, 6)
                    act.activation(TSG, TSG, ACT.Exp, scale=-1.0).then_inc(set_act, 1)
                if at(J, -1) and s == 4:
                    act.wait_ge(set_pe, 4)
                    act.activation(XDT0[DTROW:XROWS, :], DA[DTROW:XROWS, 0, 8:9], ACT.Copy).then_inc(set_act, 1)
                if at(J, -1) and s == 8:
                    act.wait_ge(set_pe, 5)
                    act.activation(TL, DA[:, 0, 40:42], ACT.Abs).then_inc(set_act, 1)
                if at(J, -1) and s == 9:
                    act.wait_ge(set_act, 9)
                    act.activation(TL, TL, ACT.Exp, scale=-1.0).then_inc(set_act, 1)
                    act.wait_ge(set_act, 10)
                    act.activation(TR, TL, ACT.Ln, bias=LOGB[:, 0:1], scale=1.0 / LOG_C).then_inc(set_act, 1)
                    act.wait_ge(set_act, 11)
                    act.activation(TR, TR, ACT.Exp, scale=-1.0).then_inc(set_act, 1)
                if at(J, -1) and s == 12:
                    act.wait_ge(set_dve, 6)
                    act.activation(TR, TL, ACT.Square, scale=1.0 / LOG_C).then_inc(set_act, 1)
                    act.wait_ge(set_act, 13)
                    act.activation(TS, TR, ACT.Square, bias=LOGB[:, 1:2]).then_inc(set_act, 1)
                if front and s == 1:
                    act.wait_ge(sg_chain, 2 * f + 1)
                    act.activation(SG[:, :, :], SG[:, :, :], ACT.Ln, bias=1.0).then_inc(sg_chain, 1)
                if front and s == 2:
                    act.wait_ge(sg_chain, 2 * f + 2)
                    act.activation(SG[:, :, :], SG[:, :, :], ACT.Exp, scale=-1.0).then_inc(sg_ready, 1)
                if front and s == 8:
                    act.wait_ge(dtp_ready, f + 1)
                    positive(act, dt_ready, f)
                    act.activation(SE[:, :, :], PPT, ACT.Abs).then_inc(sp_chain, 1)
                    act.activation(DT[:, fp], PPT, ACT.Relu).then_inc(relu_done, 1)
                if front and s == 9:
                    act.wait_ge(sp_chain, 3 * f + 1)
                    act.activation(SE[:, :, :], SE[:, :, :], ACT.Exp, scale=-1.0).then_inc(sp_chain, 1)
                    act.wait_ge(sp_chain, 3 * f + 2)
                    act.activation(SR[:, :, :], SE[:, :, :], ACT.Ln, bias=LOGB[:, 0:1], scale=1.0 / LOG_C)\
                        .then_inc(sp_chain, 1)
                if front and s == 10:
                    act.wait_ge(sp_chain, 3 * f + 3)
                    act.activation(SR[:, :, :], SR[:, :, :], ACT.Exp, scale=-1.0).then_inc(sq_e_ready, 1)
                if back and s == 11:
                    act.wait_ge(xc2_ready, k + 1)
                    act.activation(SQ2[:, :, :], XC2[:, :, :], ACT.Square).then_inc(sq2_ready, 1)
                if back and s == 12:
                    act.wait_ge(var2_ready, k + 1)
                    act.activation(LNV2[:, :], STAT2, ACT.Ln, bias=EPST[:, 0:1]).then_inc(ln2_done, 1)
                    act.wait_ge(ln2_done, k + 1)
                    positive(act, out_ready, k)
                    act.activation(RSTD2[:, :], LNV2[:, :], ACT.Exp, scale=-0.5).then_inc(rstd2_ready, 1)
                if at(J, ROUTE) and s == 11:
                    act.wait_ge(f_dve, 1)
                    act.activation(x0s, x0, ACT.Square).then_inc(f_act, 1)
                if at(J, ROUTE) and s == 12:
                    act.wait_ge(f_pe, 2)
                    act.activation(r0, PP[:, 1, 0:BATCH], ACT.Ln, bias=EPST[:, 0:1]).then_inc(f_act, 1)
                    act.wait_ge(f_act, 2)
                    act.activation(r0, r0, ACT.Exp, scale=-0.5).then_inc(f_act, 1)
                if at(J, ROUTE + 1) and s == 12:
                    act.wait_ge(f_dve, 5)
                    act.activation(WEX, TOP, ACT.Exp, bias=NMX, accum_out=WSUM).then_inc(f_act, 1)
                if norm and s == 11:
                    act.wait_ge(xc_ready, g + 1)
                    positive(act, var_ready, g)
                    act.activation(SQ[:, :, :], XC[:, :, :], ACT.Square).then_inc(sq_ready, 1)
                if main and s == 13:
                    act.wait_ge(z_clamped, J + 1)
                    positive(act, gz_ready, J)
                    act.activation(SGZ[:, :, :], GZ[:, :, :], ACT.Exp, scale=-1.0).then_inc(sgz_chain, 1)
                if norm and s == 12:
                    act.wait_ge(var_ready, g + 1)
                    act.activation(LNV[:, :], STAT, ACT.Ln, bias=EPSC[:, 0:1]).then_inc(ln_done, 1)
                    act.wait_ge(ln_done, g + 1)
                    positive(act, xn_ready, g)
                    act.activation(RSTD[:, :], LNV[:, :], ACT.Exp, scale=-0.5).then_inc(rstd_ready, 1)
                if main and s == 14:
                    act.wait_ge(sgz_chain, 2 * J + 1)
                    act.activation(SGZ[:, :, :], SGZ[:, :, :], ACT.Ln, bias=1.0).then_inc(sgz_chain, 1)
                if main and s == 15:
                    act.wait_ge(sgz_chain, 2 * J + 2)
                    act.activation(SGZ[:, :, :], SGZ[:, :, :], ACT.Exp, scale=-1.0).then_inc(sgz_ready, 1)

            def first_main():
                act.wait_ge(dt_ready, 1)
                act.wait_ge(car_saved, 4 * BATCH)
                decay(0, 0, 0, 0, 0)
                act.wait_ge(st_ready, 1)
                act.activation(CS[:, 0], ST[:, 0:T], ACT.Copy).then_inc(st_copied, 1)
                decay(0, 0, 0, 0, 1)

            run_units(act, step, before_conv=weights, first_main=first_main)

        @block.tensor
        def _(pe):
            pe.wait_ge(const_ready, 1)

            def weights():
                pe.wait_ge(ident_ready, 1)
                pe.wait_ge(set_dve, 1)
                for h in range(HALVES):
                    for k in range(TAPS):
                        last = pe.transpose(Yp[:, h, k * P:(k + 1) * P], WSC[:, h * TAPS + k], IDENT[:, :])
                last.then_inc(set_pe, 1)
                pe.wait_ge(w_loaded, 16 * N_WLOADS)
                pe.wait_ge(ln_done, 1)
                for h in range(HALVES):
                    pe.transpose(PP[:, 0, h * P:(h + 1) * P], WNAT[:, HALVES + h], IDENT[:, :])
                    pe.transpose(PP[:, 0, 256 + h * P:256 + (h + 1) * P], OPNAT[:, h * P:(h + 1) * P], IDENT[:, :])
                    pe.transpose(PP[:, 1, h * 40:h * 40 + 40], XPNAT[:, h * P:(h + 1) * P], IDENT[0:40, 0:40])
                    last = pe.transpose(PP[0:XROWS + 1, 1, 128 + h * P:256 + h * P], DTNAT[:, h], IDENT[:, :])
                last.then_inc(set_pe, 1)

            X0v = X[:, 0:BATCH * T].rearrange("p (b q t) -> p q b t", b=BATCH, q=Q)[:, :, :, 0]

            def spread_b(unit, par, n):
                before = NDVE * unit + dve_index(n)
                positive(pe, dbu_dve, before)
                pe.matmul(BB[:, 0:T], SEL[:, n], PT[:, par], start=True, stop=True).then_inc(b_ready, 1)

            def spread_b_pool(unit, par, n):
                pe.wait_ge(st_copied, STAGES_PER_UNIT * unit + stage_index("B", n))
                pe.matmul(ST[:, 0:T], SEL[:, n], PT[:, par], start=True, stop=True).then_inc(st_ready, 1)

            def spread_c(unit, par, n):
                positive(pe, st_copied, STAGES_PER_UNIT * unit + stage_index("C", n))
                pe.matmul(ST[:, 0:T], SEL[:, NS + n], PT[:, par], start=True, stop=True).then_inc(st_ready, 1)

            def step(J, par, s, main, front, back, prev, conv, norm):
                f, k, g, N = J + 1, J - 1, J + 3, NS * J + s
                fp = kp = 1 - par
                if main:
                    if s + 2 < NS and s + 2 not in POOL_STATES:
                        spread_b(J, par, s + 2)
                    elif s + 2 >= NS and front:
                        spread_b(J + 1, 1 - par, s + 2 - NS)
                if main and s >= LAG or prev and s < LAG:
                    n3 = (s - LAG) % NS
                    pe.wait_ge(m_ready, N - LAG + 1)
                    if s == LAG:
                        positive(pe, v_ready, J)
                    for h in range(HALVES):
                        last = pe.matmul(Yp[:, h, 0:T], IDENT[:, :], M[:, n3 % MRING, h],
                                         start=n3 == 0, stop=n3 == NS - 1)
                    last.then_inc(ysum_done, 1)
                if main and s == 7:
                    for h in range(HALVES):
                        pe.matmul(Yp[:, h, 0:T], DD[:, h], U[:, par, h], start=False, stop=False)
                if at(J, -2) and s == 13:
                    for h in range(HALVES):
                        last = pe.matmul(DA[:, 0, h:h + 1], WT[:, h, TAPS - 1], TKC, start=True, stop=True)
                    last.then_inc(set_pe, 1)
                if at(J, -1) and s == 3:
                    pe.wait_ge(set_dve, 5)
                    for h in range(HALVES):
                        pe.matmul(DA[0:XROWS, 0, 8:9], XPT[:, h, :], TU[:, h:h + 1], start=h == 0, stop=h == 1)
                    for h in range(HALVES):
                        last = pe.matmul(DA[:, 0, 16:32], UB[:, h], XPT[:, h, 0:NS], start=h == 0, stop=h == 1)
                    last.then_inc(set_pe, 1)
                if at(J, -1) and s == 7:
                    pe.wait_ge(set_act, 8)
                    for h in range(HALVES):
                        last = pe.matmul(DA[:, 0, 40 + h:41 + h], DTW[DTROW:XROWS + 1, h],
                                         XDT0[DTROW:XROWS + 1, :], start=True, stop=True, tile_position=(DTROW, 0))
                    last.then_inc(set_pe, 1)
                if front and s == 3:
                    pe.wait_ge(u_ready, f + 1)
                    for h in range(HALVES):
                        last = pe.matmul(PP[0:XROWS, 1, 0:T], XPT[:, h], U[:, fp, h], start=h == 0, stop=h == 1)
                    last.then_inc(xp_ready, 1)
                if back and s == 4:
                    pe.wait_ge(v_ready, k + 1)
                    if front:
                        pe.wait_ge(clamped, 2 * f + 1)
                    for h in range(HALVES):
                        last = pe.matmul(PP[:, 0, 0:T], OPT[:, h], VV[:, h], start=h == 0, stop=h == 1)
                    last.then_inc(op_ready, 1)
                if back and s == 9:
                    pe.wait_ge(x2_ready, k + 1)
                    if front:
                        pe.wait_ge(relu_done, f + 1)
                    for q in range(Q):
                        last = pe.matmul(STAT2, MEANW[:, :], unit_x(k)[:, q], start=q == 0, stop=q == Q - 1)
                    last.then_inc(mean2_ready, 1)
                if at(J, ROUTE) and s == 9:
                    for q in range(Q):
                        last = pe.matmul(PP[:, 1, 0:BATCH], MEANW[:, :], X0v[:, q], start=q == 0, stop=q == Q - 1)
                    last.then_inc(f_pe, 1)
                if at(J, ROUTE) and s == 12:
                    pe.wait_ge(z_clamped, J + 1)
                    pe.wait_ge(f_act, 1)
                    for q in range(Q):
                        last = pe.matmul(PP[:, 1, 0:BATCH], MEANW[:, :], x0s[:, q], start=q == 0, stop=q == Q - 1)
                    last.then_inc(f_pe, 1)
                if at(J, ROUTE + 1) and s == 9:
                    pe.wait_ge(f_dve, 2)
                    pe.wait_ge(ffn_loaded, 16)
                    for q in range(Q):
                        last = pe.matmul(PP[0:BATCH, 1, 0:MEM], x0[:, q], RW[:, q], start=q == 0, stop=q == Q - 1)
                    last.then_inc(f_pe, 1)
                if at(J, ROUTE + 1) and s == 14:
                    pe.wait_ge(z_clamped, J + 1)
                    pe.wait_ge(f_dve, 8)
                    pe.matmul(PP[:, 1, 0:BATCH * TOPK], ONE4[:, :], WDG.rearrange("p b k -> p (b k)"),
                              start=True, stop=True).then_inc(f_pe, 1)
                for b, q in COMBINE.get((J, s), ()) if isinstance(J, int) else ():
                    if q == 0:
                        pe.wait_ge(f_dve, (10, 11, 12, 13)[b])
                        if b == 1:
                            pe.wait_ge(comb_done, 1)
                        if b == 2:
                            pe.wait_ge(z_clamped, UNITS)
                        pe.wait_ge(g_loaded[b], 16 * TOPK)
                    for kk in range(TOPK):
                        last = pe.matmul(comb_bank(b)[:, q * P:(q + 1) * P],
                                         G[b % 2][:, kk].rearrange("p (c q) -> p q c", q=Q)[:, q],
                                         WI[:, b % 3, kk], start=kk == 0, stop=kk == TOPK - 1)
                    if q == Q - 1:
                        last.then_inc(g_used, 1)
                if main and s == 10:
                    if back:
                        pe.wait_ge(xc2_ready, k + 1)
                    elif front:
                        pe.wait_ge(relu_done, f + 1)
                    if norm:
                        pe.wait_ge(xc_ready, g + 1)
                    if at(J, ROUTE):
                        pe.wait_ge(f_dve, 1)
                    if at(J, ROUTE + 1):
                        pe.wait_ge(f_dve, 3)
                    if at(J, COMB):
                        pe.wait_ge(comb_done, 2)
                    for h in range(HALVES):
                        last = pe.matmul(PP[:, h, 0:T], WZT[:, h], unit_seq(J), start=True, stop=True)
                    last.then_inc(z_ready, 1)
                if at(J, -2) and s == 9:
                    pe.wait_ge(set_act, 4)
                if norm and s == 9:
                    if isinstance(g, int) and g < BATCH:
                        pe.wait_ge(x_first[g], 16)
                    else:
                        pe.wait_ge(x_loaded, 16 * (UNITS - BATCH))
                    if front:
                        pe.wait_ge(relu_done, f + 1)
                    positive(pe, ln_done, g)
                    for q in range(Q):
                        last = pe.matmul(STAT, MEANW[:, :], unit_x(g)[:, q], start=q == 0, stop=q == Q - 1)
                    last.then_inc(mean_ready, 1)
                if back and s == 12:
                    if main:
                        pe.wait_ge(z_clamped, J + 1)
                    pe.wait_ge(sq2_ready, k + 1)
                    for q in range(Q):
                        last = pe.matmul(STAT2, MEANW[:, :], SQ2[:, q], start=q == 0, stop=q == Q - 1)
                    last.then_inc(var2_ready, 1)
                if norm and s == 12:
                    if main:
                        pe.wait_ge(z_clamped, J + 1)
                    pe.wait_ge(sq_ready, g + 1)
                    for q in range(Q):
                        last = pe.matmul(STAT, MEANW[:, :], SQ[:, q], start=q == 0, stop=q == Q - 1)
                    last.then_inc(var_ready, 1)
                if conv and s >= 13:
                    if s == 13:
                        pe.wait_ge(xn_ready, J + 3)
                        if back:
                            pe.wait_ge(ln2_done, k + 1)
                        elif main:
                            pe.wait_ge(z_clamped, J + 1)
                        elif front:
                            pe.wait_ge(relu_done, f + 1)
                    for m in range((s - 13) * 3, min((s - 13) * 3 + 3, HALVES * TAPS)):
                        h, tap = m // TAPS, m % TAPS
                        if m == TAPS:
                            if norm:
                                pe.wait_ge(ln_done, g + 1)
                            else:
                                pe.wait_ge(f_act, 2)
                        last = pe.matmul(PP[:, h, 0:T], WT[:, h, tap], XN[:, ds((J + 2) * SLOT + tap, T)],
                                         start=tap == 0, stop=tap == TAPS - 1)
                        if tap == TAPS - 1:
                            last.then_inc(conv_ready, 1)
                if main and s + 3 in POOL_STATES:
                    spread_b_pool(J, par, s + 3)
                if main and s < NS - 2:
                    spread_c(J, par, s + 2)
                elif main and front:
                    spread_c(J + 1, 1 - par, s + 2 - NS)
                if front and s == 7:
                    pe.wait_ge(hi_ready, f + 1)
                    if back:
                        pe.wait_ge(x2_ready, k + 1)
                    for h in range(HALVES):
                        if h == 1:
                            pe.wait_ge(parts_ready, f + 1)
                        last = pe.matmul(PP[:, h, 0:T], DTW[DTROW:XROWS + 1, h], XDT[DTROW:XROWS + 1, :],
                                         start=True, stop=True, tile_position=(DTROW, 0))
                    last.then_inc(dtp_ready, 1)

            def first_main():
                pe.wait_ge(parts_ready, 1)
                pe.wait_ge(sel_ready, 1)
                spread_b(0, 0, 0)
                spread_c(0, 0, 0)
                spread_c(0, 0, 1)
                spread_b(0, 0, 1)

            run_units(pe, step, before_conv=weights, first_main=first_main)

        @block.vector
        def _(dve):
            dve.wait_ge(wc_loaded, 32)
            for h in range(HALVES):
                for k in range(TAPS):
                    last = dve.tensor_scalar(WSC[:, h * TAPS + k], WNAT[:, h], CW[:, h, k:k + 1], None, ALU.mult)
            last.then_inc(set_dve, 1)

            def weights():
                dve.wait_ge(w_loaded, 16 * N_WLOADS)
                dve.wait_ge(ident_ready, 1)
                for h in range(HALVES):
                    dve.tensor_scalar(DD[:, h], IDENT[:, :], DV[:, h:h + 1], None, ALU.mult)
                dve.memset(LESS[:, :], 0.0).then_inc(less_set, 1)
                dve.wait_ge(less_set, 1)
                dve.memset(LESS[BC:2 * BC, 0:1], -1.0)
                dve.memset(LESS[2 * BC:3 * BC, :], -1.0).then_inc(less_set, 1)
                dve.wait_ge(less_set, 2)

            X0v = X[:, 0:BATCH * T].rearrange("p (b q t) -> p q b t", b=BATCH, q=Q)[:, :, :, 0]

            def weigh(b):
                dve.tensor_tensor(WI[:, b % 3], IDENT[:, :].unsqueeze(1).broadcast_to([P, TOPK, P]),
                                  WBC[:, b * TOPK:(b + 1) * TOPK].unsqueeze(2).broadcast_to([P, TOPK, P]),
                                  ALU.mult).then_inc(f_dve, 1)

            def add_routed(b):
                ps = comb_bank(b).rearrange("p (q t) -> p q t", q=Q)
                dve.wait_ge(g_used, b + 1)
                o0 = unit_seq(b).rearrange("p (q t) -> p q t", q=Q)
                o1 = unit_seq(BATCH + b).rearrange("p (q t) -> p q t", q=Q)
                dve.tensor_tensor(o0[:, :, 1:TOK], unit_x(b)[:, :, 1:TOK], ps[:, :, 0:TOK - 1], ALU.add)
                rest = MT - (TOK - 1)
                dve.tensor_tensor(o1[:, :, 0:rest], unit_x(BATCH + b)[:, :, 0:rest], ps[:, :, TOK - 1:MT], ALU.add)\
                    .then_inc(comb_done, 1)

            def drive(unit, par, n, N):
                positive(dve, m_ready, N - HRING + 1)
                dve.wait_ge(b_ready, NDVE * unit + dve_index(n) + 1)
                dve.tensor_tensor(HB[:, n % HRING], DTU[:, par], over_halves(BB[:, 0:T]), ALU.mult)\
                    .then_inc(dbu_dve, 1)

            def step(J, par, s, main, front, back, prev, conv, norm):
                f, k, g, N = J + 1, J - 1, J + 3, NS * J + s
                fp = kp = 1 - par
                if back and s == 1:
                    dve.wait_ge(sgz_ready, k + 1)
                    dve.tensor_tensor(GZ[:, :, :], GZ[:, :, :], SGZ[:, :, :], ALU.mult).then_inc(gz_ready, 1)
                if back and s == LAG:
                    dve.wait_ge(ysum_done, NS * (k + 1))
                    dve.wait_ge(gz_ready, k + 1)
                    positive(dve, op_ready, k)
                    dve.tensor_tensor(VV[:, :, :], Yp[:, :, 0:T], GZ[:, :, :], ALU.mult).then_inc(v_ready, 1)
                if s % GRP == 1 and (main and s > 1 or prev and s == 1):
                    grp = (s // GRP - 1) % GRP
                    unit = J if s > 1 else J - 1
                    dve.wait_ge(scan_done, 2 * (N - 1))
                    dve.tensor_copy(CAR[:, ds((unit + BATCH) * NS * HALVES + grp * GRP * HALVES, GRP * HALVES)]
                                    .rearrange("p (n h) -> p n h", h=HALVES),
                                    HB[:, (grp % 2) * GRP:(grp % 2) * GRP + GRP, :, T - 1]).then_inc(car_saved, 1)
                if main:
                    if s + 1 < NS and s + 1 not in POOL_STATES:
                        drive(J, par, s + 1, N + 1)
                    elif s + 1 == NS and front:
                        dve.wait_ge(dtu_ready, J + 2)
                        drive(J + 1, 1 - par, 0, N + 1)
                if front and s == 6:
                    dve.wait_ge(hi_ready, f + 1)
                    dve.scalar_tensor_tensor(out=PP[0:DTROW, 1, 0:T], in0=PART[:, :], scalar=LESS[:, 0:1],
                                             in1=PP[0:DTROW, 1, 0:T], op0=ALU.mult, op1=ALU.add)\
                        .then_inc(res_ready, 1)
                if back and s == 10:
                    dve.wait_ge(mean2_ready, k + 1)
                    positive(dve, out_ready, k)
                    dve.tensor_tensor(XC2[:, :, :], unit_x(k), over_q(STAT2), ALU.subtract).then_inc(xc2_ready, 1)
                if norm and s == 10:
                    dve.wait_ge(mean_ready, g + 1)
                    positive(dve, xn_ready, g)
                    dve.tensor_tensor(XC[:, :, :], unit_x(g), over_q(STAT), ALU.subtract).then_inc(xc_ready, 1)
                if front and s == 13:
                    dve.wait_ge(r2_ready, 2 * f + 1)
                    dve.scalar_tensor_tensor(out=SE[:, :, :], in0=SR[:, :, :], scalar=LOG_D, in1=SE[:, :, :],
                                             op0=ALU.add, op1=ALU.mult).then_inc(m1_done, 1)
                if front and s == 3:
                    dve.wait_ge(clamped, 2 * f + 2)
                    dve.wait_ge(sg_ready, f + 1)
                    dve.tensor_tensor(U[:, fp], U[:, fp], SG[:, :, :], ALU.mult).then_inc(u_ready, 1)
                if main:
                    if s in POOL_STATES:
                        dve.wait_ge(dbu_pool, NPOOL * J + pool_index(s) + 1)
                    else:
                        dve.wait_ge(dbu_dve, NDVE * J + dve_index(s) + 1)
                    dve.wait_ge(car_saved, 4 * J + s // GRP + 1)
                    for h in range(HALVES):
                        dve.wait_ge(da_ready, 2 * N + h + 1)
                        dve.tensor_tensor_scan(HB[:, s % HRING, h], DA[:, h, 0:T], HB[:, s % HRING, h],
                                               CAR[:, ds(J * NS * HALVES + s * HALVES + h, 1)],
                                               ALU.mult, ALU.add).then_inc(scan_done, 1)
                if at(J, -1) and s == 0:
                    dve.wait_ge(set_pe, 3)
                    dve.tensor_tensor(TUC, DA[:, 0, 0:2], CB_[:, :], ALU.add).then_inc(set_dve, 1)
                    dve.wait_ge(set_dve, 2)
                    dve.tensor_scalar(TUC, TUC, NEG_LIMIT, None, ALU.max).then_inc(set_dve, 1)
                if at(J, -1) and s == 3:
                    dve.wait_ge(set_act, 7)
                    dve.tensor_tensor(TU, TUC, TSG, ALU.mult).then_inc(set_dve, 1)
                    dve.wait_ge(set_dve, 4)
                    dve.tensor_copy(UB, TU.unsqueeze(2).broadcast_to([P, HALVES, P])).then_inc(set_dve, 1)
                if at(J, -1) and s == 10:
                    dve.wait_ge(set_act, 12)
                    dve.tensor_tensor(TL, TL, TR, ALU.mult).then_inc(set_dve, 1)
                if at(J, -1) and s == 13:
                    dve.wait_ge(set_act, 14)
                    dve.scalar_tensor_tensor(out=TL, in0=TR, scalar=LOG_D, in1=TL, op0=ALU.add, op1=ALU.mult)\
                        .then_inc(set_dve, 1)
                    dve.wait_ge(set_dve, 7)
                    dve.scalar_tensor_tensor(out=TL, in0=TS, scalar=LOG_H, in1=TL, op0=ALU.add, op1=ALU.mult)\
                        .then_inc(set_dve, 1)
                    dve.wait_ge(set_dve, 8)
                    dve.scalar_tensor_tensor(out=TDT, in0=DA[:, 0, 40:42], scalar=0.0, in1=TL, op0=ALU.max,
                                             op1=ALU.add).then_inc(set_dve, 1)
                    dve.wait_ge(set_dve, 9)
                    dve.tensor_tensor(TDU, TDT, TU, ALU.mult).then_inc(set_dve, 1)
                    dve.wait_ge(set_dve, 10)
                    for h in range(HALVES):
                        last = dve.tensor_scalar(CAR[:, 0:NS * HALVES].rearrange("p (n h) -> p n h", h=HALVES)
                                                 [:, :, h], DA[:, 0, 16:32], TDU[:, h:h + 1], None, ALU.mult)
                    last.then_inc(set_dve, 1)
                    dve.wait_ge(set_dve, 11)
                    dve.tensor_copy(CAR[:, NS * HALVES:BATCH * NS * HALVES].rearrange("p (b n) -> p b n",
                                                                                      b=BATCH - 1),
                                    CAR[:, 0:NS * HALVES].unsqueeze(1).broadcast_to([P, BATCH - 1, NS * HALVES]))\
                        .then_inc(car_saved, 4 * BATCH)
                if at(J, ROUTE) and s == 10:
                    dve.wait_ge(f_pe, 1)
                    dve.tensor_tensor(x0, X0v, PP[:, 1, 0:BATCH].unsqueeze(1).broadcast_to([P, Q, BATCH]),
                                      ALU.subtract).then_inc(f_dve, 1)
                if at(J, ROUTE + 1) and s == 1:
                    dve.wait_ge(f_act, 3)
                    dve.tensor_tensor(x0, x0, r0.unsqueeze(1).broadcast_to([P, Q, BATCH]), ALU.mult)\
                        .then_inc(f_dve, 1)
                if at(J, ROUTE + 1) and s == 10:
                    dve.wait_ge(f_pe, 3)
                    dve.tensor_copy(SCO, PP[0:BATCH, 1, 0:MEM]).then_inc(f_dve, 1)
                    dve.wait_ge(f_dve, 3)
                    dve.max(TOP, SCO).then_inc(f_dve, 1)
                    dve.wait_ge(f_dve, 4)
                    dve.tensor_scalar(NMX, TOP[:, 0:1], -1.0, None, ALU.mult).then_inc(f_dve, 1)
                    dve.max_index(IDX[:, :], TOP, SCO).then_inc(idx_ready, 1)
                if at(J, ROUTE + 1) and s == 13:
                    dve.wait_ge(f_act, 4)
                    dve.reciprocal(WRC, WSUM).then_inc(f_dve, 1)
                    dve.wait_ge(f_dve, 6)
                    dve.tensor_scalar(WNM, WEX, WRC, None, ALU.mult).then_inc(f_dve, 1)
                    dve.wait_ge(f_dve, 7)
                    dve.tensor_tensor(WDG, IDENT[0:BATCH, 0:BATCH].unsqueeze(2).broadcast_to([BATCH, BATCH, TOPK]),
                                      WNM.unsqueeze(1).broadcast_to([BATCH, BATCH, TOPK]), ALU.mult)\
                        .then_inc(f_dve, 1)
                if at(J, ROUTE + 1) and s == 15:
                    dve.wait_ge(f_pe, 4)
                    dve.tensor_copy(WBC, PP[:, 1, 0:BATCH * TOPK]).then_inc(f_dve, 1)
                if at(J, COMB) and s < BATCH - 1:
                    dve.wait_ge(f_dve, 9)
                    weigh(s)
                if isinstance(J, int) and (J, s) in ADD:
                    add_routed(ADD[(J, s)])
                if at(J, COMB) and s == 6:
                    weigh(3)
                if front and s == 0:
                    for h in range(HALVES):
                        dve.wait_ge(conv_ready, 2 * f + h + 1)
                        dve.tensor_scalar(U[:, fp, h], PP[:, h, 0:T], CB_[:, h:h + 1], NEG_LIMIT, ALU.add, ALU.max)\
                            .then_inc(clamped, 1)
                if back and s == 5:
                    dve.wait_ge(op_ready, k + 1)
                    for r1 in range(2):
                        xr = by_row_parity(unit_x(k), r1)
                        last = dve.tensor_tensor(xr, xr, seq_rows(PP[:, 0, 0:T], r1), ALU.add)
                    last.then_inc(x2_ready, 1)
                if front and s == 6:
                    dve.wait_ge(mid_ready, f + 1)
                    dve.scalar_tensor_tensor(out=PT[:, fp], in0=PART[:, :], scalar=LESS[:, 1:2],
                                             in1=PP[0:DTROW, 1, 0:T], op0=ALU.mult, op1=ALU.add)\
                        .then_inc(parts_ready, 1)
                if main and s == 11:
                    dve.wait_ge(z_ready, J + 1)
                    if back:
                        dve.wait_ge(v_ready, k + 1)
                    dve.tensor_scalar(GZ[:, :, :], PPT, NEG_LIMIT, None, ALU.max).then_inc(z_clamped, 1)
                if front and s == 13:
                    dve.wait_ge(r2_ready, 2 * f + 2)
                    dve.wait_ge(m1_done, 2 * f + 1)
                    dve.scalar_tensor_tensor(out=SE[:, :, :], in0=SS[:, :, :], scalar=LOG_H, in1=SE[:, :, :],
                                             op0=ALU.add, op1=ALU.mult).then_inc(m1_done, 1)
                    dve.wait_ge(relu_done, f + 1)
                    dve.wait_ge(m1_done, 2 * f + 2)
                    dve.tensor_tensor(DT[:, fp], DT[:, fp], SE[:, :, :], ALU.add).then_inc(dt_ready, 1)

            def first_main():
                dve.wait_ge(dtu_ready, 1)
                drive(0, 0, 0, 0)

            run_units(dve, step, before_conv=weights, first_main=first_main)


_NAMES = ["x", "L0_conv_global_token", "L0_conv_in_proj_w", "L0_conv_conv_w", "L0_conv_conv_b",
          "L0_conv_x_proj_w", "L0_conv_dt_proj_w", "L0_conv_dt_proj_b", "L0_conv_A_log", "L0_conv_D",
          "L0_conv_out_proj_w", "L0_ffn_memory_tokens", "L0_ffn_memory_router"]


def kernel(**inputs):
    import numpy as np
    import concourse.bacc as bacc
    from concourse.bass_utils import run_bass_kernel_spmd as run

    nc = bacc.Bacc("TRN2", target_bir_lowering=False, num_devices=1)
    arrays, args = {}, []
    for name in _NAMES:
        a = np.ascontiguousarray(inputs[name])
        arrays[f"in_{name}"] = a
        args.append(nc.dram_tensor(f"in_{name}", a.shape, mybir.dt.from_np(a.dtype), kind="ExternalInput").ap())
    shape = inputs["x"].shape
    result = nc.dram_tensor("out_0", shape, F32, kind="ExternalOutput").ap()
    build(nc, *args, result)
    r = run(nc, [arrays], core_ids=[0])
    return r.results[0]["out_0"]
```
